# Optimizing a Trainium2 kernel written in Bass

```python
import numpy as np
import jax
import jax.numpy as jnp

def _softmax(x, axis=-1):
    return jax.nn.softmax(x, axis=axis)

def _gelu(x):
    return jax.nn.gelu(x, approximate=True)

def _silu(x):
    return jax.nn.silu(x)

def _sigmoid(x):
    return jax.nn.sigmoid(x)

def _layernorm(x, axis=-1, eps=1e-05):
    m = jnp.mean(x, axis=axis, keepdims=True)
    v = jnp.var(x, axis=axis, keepdims=True)
    return (x - m) / jnp.sqrt(v + eps)

def _scatter_add(tgt, idx, src, axis=0):
    return tgt.at[idx].add(src)

def _segment_sum(src, seg, n):
    return jax.ops.segment_sum(src, seg, n)
kernel_name = 'mk_macaron_d1_jaxref_r2_a18db4'

def setup_inputs(seed: int=0):
    np.random.seed(seed)
    _w = jnp.asarray

    def _L0_attn_setup():
        import jax, jax.numpy as jnp
        import numpy as np
        B, S, D = (2, 512, 512)
        NH = 8
        QK = D // 2
        V = D
        DQK = QK // NH
        DV = V // NH
        CAP = 15.0
        EPS = 1e-06

        def soft_cap(t, cap=CAP):
            return cap * jnp.tanh(t / cap)

        def _mlstm_forward(x, Wq, Wk, Wv, Wog, Wi, bi, Wf, bf, ln_w, ln_b, Wout):
            Bx, Sx, _ = x.shape
            q = (x @ Wq.T).reshape(Bx, Sx, NH, DQK)
            k = (x @ Wk.T).reshape(Bx, Sx, NH, DQK)
            v = (x @ Wv.T).reshape(Bx, Sx, NH, DV)
            o_preact = x @ Wog.T
            i_pre = soft_cap(x @ Wi.T + bi)
            f_pre = soft_cap(x @ Wf.T + bf)
            qT = jnp.moveaxis(q, 1, 0)
            kT = jnp.moveaxis(k, 1, 0)
            vT = jnp.moveaxis(v, 1, 0)
            iT = jnp.moveaxis(i_pre, 1, 0)
            fT = jnp.moveaxis(f_pre, 1, 0)
            qk_scale = DQK ** (-0.5)

            def step(carry, inp):
                C, n, m = carry
                q_t, k_t, v_t, i_t, f_t = inp
                m_new = jnp.maximum(f_t + m, i_t)
                f_act = jnp.exp(f_t + m - m_new)
                i_act = jnp.exp(i_t - m_new)
                C = f_act[..., None, None] * C + i_act[..., None, None] * (k_t[..., :, None] * v_t[..., None, :])
                n = f_act[..., None] * n + i_act[..., None] * k_t
                qs = q_t * qk_scale
                num = jnp.einsum('bhk,bhkv->bhv', qs, C)
                qn = jnp.einsum('bhk,bhk->bh', qs, n)
                denom = jnp.maximum(jnp.abs(qn), jnp.exp(-m_new)) + 1e-06
                h_t = num / denom[..., None]
                return ((C, n, m_new), h_t)
            C0 = jnp.zeros((Bx, NH, DQK, DV), x.dtype)
            n0 = jnp.zeros((Bx, NH, DQK), x.dtype)
            m0 = jnp.zeros((Bx, NH), x.dtype)
            _, hs = jax.lax.scan(step, (C0, n0, m0), (qT, kT, vT, iT, fT))
            h = jnp.moveaxis(hs, 0, 1).reshape(Bx, Sx, NH * DV)
            mu = jnp.mean(h, axis=-1, keepdims=True)
            var = jnp.mean((h - mu) ** 2, axis=-1, keepdims=True)
            h_norm = (h - mu) * jax.lax.rsqrt(var + EPS) * ln_w + ln_b
            h_out = jax.nn.sigmoid(o_preact) * h_norm
            y = h_out @ Wout.T
            return y
        key = jax.random.key(seed)
        ks = jax.random.split(key, 12)
        sc = 0.02
        return {'x': jax.random.normal(ks[0], (B, S, D), jnp.float32), 'Wq': jax.random.normal(ks[1], (QK, D), jnp.float32) * sc, 'Wk': jax.random.normal(ks[2], (QK, D), jnp.float32) * sc, 'Wv': jax.random.normal(ks[3], (V, D), jnp.float32) * sc, 'Wog': jax.random.normal(ks[4], (V, D), jnp.float32) * sc, 'Wi': jax.random.normal(ks[5], (NH, D), jnp.float32) * sc, 'bi': jax.random.normal(ks[6], (NH,), jnp.float32) * sc, 'Wf': jax.random.normal(ks[7], (NH, D), jnp.float32) * sc, 'bf': jax.random.normal(ks[8], (NH,), jnp.float32) * sc + 3.0, 'ln_w': jnp.ones((NH * DV,), jnp.float32), 'ln_b': jnp.zeros((NH * DV,), jnp.float32), 'Wout': jax.random.normal(ks[9], (D, V), jnp.float32) * sc}
    _L0_attn_in = _L0_attn_setup()

    def _L0_ffn_setup():
        import jax, jax.numpy as jnp
        import numpy as np
        D_MODEL, D_FF, RANK = (512, 2048, 128)
        B, S = (4, 2048)
        key = jax.random.key(seed)
        ks = jax.random.split(key, 7)
        return {'x': jax.random.normal(ks[0], (B, S, D_MODEL), dtype=jnp.float32), 'U1': jax.random.normal(ks[1], (D_MODEL, RANK), dtype=jnp.float32) * 0.02, 'V1': jax.random.normal(ks[2], (RANK, D_FF), dtype=jnp.float32) * 0.02, 'b1': jnp.zeros((D_FF,), dtype=jnp.float32), 'U2': jax.random.normal(ks[3], (D_FF, RANK), dtype=jnp.float32) * 0.02, 'V2': jax.random.normal(ks[4], (RANK, D_MODEL), dtype=jnp.float32) * 0.02, 'b2': jnp.zeros((D_MODEL,), dtype=jnp.float32)}
    _L0_ffn_in = _L0_ffn_setup()
    _d = {'L0_attn_x': _L0_attn_in['x'], 'L0_attn_Wq': _L0_attn_in['Wq'], 'L0_attn_Wk': _L0_attn_in['Wk'], 'L0_attn_Wv': _L0_attn_in['Wv'], 'L0_attn_Wog': _L0_attn_in['Wog'], 'L0_attn_Wi': _L0_attn_in['Wi'], 'L0_attn_bi': _L0_attn_in['bi'], 'L0_attn_Wf': _L0_attn_in['Wf'], 'L0_attn_bf': _L0_attn_in['bf'], 'L0_attn_ln_w': _L0_attn_in['ln_w'], 'L0_attn_ln_b': _L0_attn_in['ln_b'], 'L0_attn_Wout': _L0_attn_in['Wout'], 'L0_ffn_U1': _L0_ffn_in['U1'], 'L0_ffn_V1': _L0_ffn_in['V1'], 'L0_ffn_b1': _L0_ffn_in['b1'], 'L0_ffn_U2': _L0_ffn_in['U2'], 'L0_ffn_V2': _L0_ffn_in['V2'], 'L0_ffn_b2': _L0_ffn_in['b2']}
    _x0 = _d['L0_attn_x']
    _d['L0_attn_x'] = jax.random.normal(jax.random.fold_in(jax.random.key(seed), 1), (8, 1024, 512), dtype=_x0.dtype)
    del _x0
    return _d

def reference(L0_attn_x, L0_attn_Wq, L0_attn_Wk, L0_attn_Wv, L0_attn_Wog, L0_attn_Wi, L0_attn_bi, L0_attn_Wf, L0_attn_bf, L0_attn_ln_w, L0_attn_ln_b, L0_attn_Wout, L0_ffn_U1, L0_ffn_V1, L0_ffn_b1, L0_ffn_U2, L0_ffn_V2, L0_ffn_b2):

    def _L0_attn_ref(x, Wq, Wk, Wv, Wog, Wi, bi, Wf, bf, ln_w, ln_b, Wout):
        import jax, jax.numpy as jnp
        import numpy as np
        B, S, D = (2, 512, 512)
        NH = 8
        QK = D // 2
        V = D
        DQK = QK // NH
        DV = V // NH
        CAP = 15.0
        EPS = 1e-06

        def soft_cap(t, cap=CAP):
            return cap * jnp.tanh(t / cap)

        def _mlstm_forward(x, Wq, Wk, Wv, Wog, Wi, bi, Wf, bf, ln_w, ln_b, Wout):
            Bx, Sx, _ = x.shape
            q = (x @ Wq.T).reshape(Bx, Sx, NH, DQK)
            k = (x @ Wk.T).reshape(Bx, Sx, NH, DQK)
            v = (x @ Wv.T).reshape(Bx, Sx, NH, DV)
            o_preact = x @ Wog.T
            i_pre = soft_cap(x @ Wi.T + bi)
            f_pre = soft_cap(x @ Wf.T + bf)
            qT = jnp.moveaxis(q, 1, 0)
            kT = jnp.moveaxis(k, 1, 0)
            vT = jnp.moveaxis(v, 1, 0)
            iT = jnp.moveaxis(i_pre, 1, 0)
            fT = jnp.moveaxis(f_pre, 1, 0)
            qk_scale = DQK ** (-0.5)

            def step(carry, inp):
                C, n, m = carry
                q_t, k_t, v_t, i_t, f_t = inp
                m_new = jnp.maximum(f_t + m, i_t)
                f_act = jnp.exp(f_t + m - m_new)
                i_act = jnp.exp(i_t - m_new)
                C = f_act[..., None, None] * C + i_act[..., None, None] * (k_t[..., :, None] * v_t[..., None, :])
                n = f_act[..., None] * n + i_act[..., None] * k_t
                qs = q_t * qk_scale
                num = jnp.einsum('bhk,bhkv->bhv', qs, C)
                qn = jnp.einsum('bhk,bhk->bh', qs, n)
                denom = jnp.maximum(jnp.abs(qn), jnp.exp(-m_new)) + 1e-06
                h_t = num / denom[..., None]
                return ((C, n, m_new), h_t)
            C0 = jnp.zeros((Bx, NH, DQK, DV), x.dtype)
            n0 = jnp.zeros((Bx, NH, DQK), x.dtype)
            m0 = jnp.zeros((Bx, NH), x.dtype)
            _, hs = jax.lax.scan(step, (C0, n0, m0), (qT, kT, vT, iT, fT))
            h = jnp.moveaxis(hs, 0, 1).reshape(Bx, Sx, NH * DV)
            mu = jnp.mean(h, axis=-1, keepdims=True)
            var = jnp.mean((h - mu) ** 2, axis=-1, keepdims=True)
            h_norm = (h - mu) * jax.lax.rsqrt(var + EPS) * ln_w + ln_b
            h_out = jax.nn.sigmoid(o_preact) * h_norm
            y = h_out @ Wout.T
            return y
        return _mlstm_forward(x, Wq, Wk, Wv, Wog, Wi, bi, Wf, bf, ln_w, ln_b, Wout)

    def _L0_ffn_ref(x, U1, V1, b1, U2, V2, b2):
        import jax, jax.numpy as jnp
        import numpy as np
        D_MODEL, D_FF, RANK = (512, 2048, 128)
        B, S = (4, 2048)
        P = jnp.einsum('bsd,dr->bsr', x, U1)
        H = jax.nn.gelu(jnp.einsum('bsr,rf->bsf', P, V1) + b1)
        Q = jnp.einsum('bsf,fr->bsr', H, U2)
        return jnp.einsum('bsr,rd->bsd', Q, V2) + b2
    x = L0_attn_x
    x = x + 0.5 * _L0_ffn_ref(_layernorm(x, axis=-1), L0_ffn_U1, L0_ffn_V1, L0_ffn_b1, L0_ffn_U2, L0_ffn_V2, L0_ffn_b2)
    x = x + _L0_attn_ref(_layernorm(x, axis=-1), L0_attn_Wq, L0_attn_Wk, L0_attn_Wv, L0_attn_Wog, L0_attn_Wi, L0_attn_bi, L0_attn_Wf, L0_attn_bf, L0_attn_ln_w, L0_attn_ln_b, L0_attn_Wout)
    x = x + 0.5 * _L0_ffn_ref(_layernorm(x, axis=-1), L0_ffn_U1, L0_ffn_V1, L0_ffn_b1, L0_ffn_U2, L0_ffn_V2, L0_ffn_b2)
    return x

_drawn_inputs = setup_inputs


def setup_inputs(seed=0):
    import zlib

    import numpy as np

    out = dict(_drawn_inputs(seed))
    spreads = {'L0_attn_ln_w': (1.0, 0.2),
     'L0_attn_ln_b': (0.0, 0.345),
     'L0_ffn_b1': (0.0, 0.834),
     'L0_ffn_b2': (0.0, 0.1)}
    factors = {'L0_attn_bi': 8.0,
     'L0_attn_bf': 64.0,
     'L0_attn_Wf': 5.913,
     'L0_ffn_U1': 4.989,
     'L0_ffn_V1': 5.02}
    for name, (base, spread) in spreads.items():
        noise = np.random.default_rng([zlib.crc32(name.encode()), seed]).standard_normal(out[name].shape)
        drawn = base * np.exp(spread * noise) if base else spread * noise
        out[name] = jnp.asarray(drawn.astype(out[name].dtype))
    for name, factor in factors.items():
        out[name] = (out[name] * factor).astype(out[name].dtype)
    return out
```

```python
from contextlib import ExitStack

import concourse.bass as bass
from concourse import mybir

P = 128
F32 = mybir.dt.float32
F32R = mybir.dt.float32r
ALU = mybir.AluOpType
ACT = mybir.ActivationFunctionType

LN_EPS = 1e-5
CELL_EPS = 1e-6
CAP = 15.0


class At:

    def __init__(self, pair, offset):
        self.pair, self.offset = pair, offset

    def __add__(self, k):
        return At(self.pair, self.offset + k)

    @property
    def parity(self):
        return self.offset % 2

    def count(self, per_step, more=0):
        return self.pair * (2 * per_step) + (self.offset * per_step + more)

    def turn(self):
        return self.pair + self.offset // 2


def as_f32(ap):
    return ap.bitcast(F32)


def ffn_phase(nc, name, x_in, x_out, weights):
    T, D = x_in.shape
    TOK = 512
    TILES = TOK // P
    KD = D // P
    FT = weights["V1"].shape[1] // P
    NB = T // TOK
    RING = 4
    LAG = 3
    STATS_AT, NORM_AT, TURN_AT = 0, 5, 10
    assert NB % 2 == 0 and NB >= 4 and FT == 16 and KD == 4

    src = x_in.rearrange("(n p j) d -> n p j d", p=P, j=TILES)
    dst = x_out.rearrange("(n p j) d -> n p j d", p=P, j=TILES)

    with ExitStack() as ctx:
        def sb(label, shape, dt=F32):
            return ctx.enter_context(nc.sbuf_tensor(f"{name}_{label}", shape, dt))

        def sem(label):
            return ctx.enter_context(nc.semaphore(f"{name}_{label}"))

        x_ld = sb("x_ld", [P, 2, TILES, D])
        xb = sb("xb", [P, 2, TILES, D])
        xn = sb("xn", [P, TILES, D])
        xt_hi = sb("xt_hi", [P, KD, TOK], F32R)
        xt_lo = sb("xt_lo", [P, KD, TOK], F32R)
        y_out = sb("y_out", [P, TILES, D])
        p_hi, p_lo = sb("p_hi", [P, TOK], F32R), sb("p_lo", [P, TOK], F32R)
        q_hi, q_lo = sb("q_hi", [P, TOK], F32R), sb("q_lo", [P, TOK], F32R)
        h = sb("h", [P, RING, TOK])
        h_hi, h_lo = sb("h_hi", [P, RING, TOK], F32R), sb("h_lo", [P, RING, TOK], F32R)
        stats = sb("stats", [P, TILES, 6])
        mv = sb("mv", [P, TILES, 2])
        veps = sb("veps", [P, TILES])
        rstd = sb("rstd", [P, TILES])

        to_bank = [ctx.enter_context(nc.psum_tensor(f"{name}_to{i}", [P, 512], F32)) for i in range(2)]
        p_bank = ctx.enter_context(nc.psum_tensor(f"{name}_pb", [P, TOK], F32))
        q_bank = ctx.enter_context(nc.psum_tensor(f"{name}_qb", [P, TOK], F32))
        h_bank = [ctx.enter_context(nc.psum_tensor(f"{name}_hb{i}", [P, TOK], F32)) for i in range(RING)]

        loaded = [sem("loaded0"), sem("loaded1")]
        stats_raw, stats_done, veps_done, rstd_done = sem("stats_raw"), sem("stats_done"), sem("veps_done"), sem("rstd_done")
        xn_done, xb_done = sem("xn_done"), sem("xb_done")
        turned, xt_hi_done, xt_lo_done = sem("turned"), sem("xt_hi_done"), sem("xt_lo_done")
        p_done, p_hi_done, p_lo_done = sem("p_done"), sem("p_hi_done"), sem("p_lo_done")
        h_done, gelu_done, h_hi_done, h_lo_done = sem("h_done"), sem("gelu_done"), sem("h_hi_done"), sem("h_lo_done")
        h_used, q_hi_done, q_lo_done = sem("h_used"), sem("q_hi_done"), sem("q_lo_done")
        o_done, y_done, stored = sem("o_done"), sem("y_done"), sem("stored")

        MATRICES = ("U1", "V1", "U2", "V2")
        w = {k: (sb(f"{k}_hi", weights[k].shape, F32R), sb(f"{k}_lo", weights[k].shape, F32R)) for k in MATRICES}
        (u1_hi, u1_lo), (v1_hi, v1_lo), (u2_hi, u2_lo), (v2_hi, v2_lo) = (w[k] for k in MATRICES)
        w_rounded, w_split = sem("w_rounded"), sem("w_split")
        b1, b2_half, minus_half, ident = weights["b1"], weights["b2_half"], weights["minus_half"], weights["ident"]

        block = ctx.enter_context(nc.Block())

        def steps(eng, front, step):
            front(At(0, 0))
            step(At(0, 0), True)
            with eng.Fori(0, NB // 2 - 1) as pair:
                for u in (1, 2):
                    step(At(pair, u), True)
            step(At(0, NB - 1), False)

        @block.sync
        def _(sp):
            def load(n):
                sp.dma_start(x_ld[:, n.parity], src_of(n, src)).then_inc(loaded[n.parity], 16)

            def src_of(n, view):
                i = n.pair * 2 + n.offset
                return view[bass.ds(i, 1)].rearrange("a p j d -> (a p) j d")

            def step(n, ahead):
                if ahead:
                    sp.wait_ge(xn_done, n.count(TILES, TILES))
                    sp.wait_ge(xb_done, n.count(TILES, TILES))
                    load(n + 2)
                sp.wait_ge(y_done, n.count(TILES, TILES))
                sp.dma_start(src_of(n, dst), y_out[:, :, :]).then_inc(stored, 16)

            load(At(0, 0))
            load(At(0, 1))
            with sp.Fori(0, NB // 2 - 1) as pair:
                for u in range(2):
                    step(At(pair, u), True)
            step(At(0, NB - 2), False)
            step(At(0, NB - 1), False)
            sp.wait_ge(stored, 16 * NB)

        @block.gpsimd
        def _(pool):
            def front(n, first=False):
                pool.wait_ge(stats_done, n.count(TILES, TILES))
                nc.gpsimd.tensor_tensor(veps[:, :], mv[:, :, 1], weights["ln_eps"][:, 0:TILES], ALU.add).then_inc(veps_done, 1)
                pool.wait_ge(veps_done, n.count(1, 1))
                nc.gpsimd.tensor_tensor(rstd[:, :], veps[:, :], minus_half[:, 0:TILES], ALU.pow).then_inc(rstd_done, 1)
                if not first:
                    pool.wait_ge(y_done, (n + -1).count(TILES))
                for j in range(TILES):
                    nc.gpsimd.tensor_tensor(xb[:, n.parity, j], x_ld[:, n.parity, j], b2_half[:, :], ALU.add)\
                        .then_inc(xb_done, 1)

            front(At(0, 0), first=True)
            front(At(0, 1), first=True)
            with pool.Fori(0, NB // 2 - 1) as pair:
                for u in (2, 3):
                    front(At(pair, u))

        @block.scalar
        def _(act):
            def turn(n, k):
                act.wait_ge(turned, n.count(KD, k + 1))
                nc.scalar.activation(xt_hi[:, k], to_bank[k % 2][:, :], ACT.Copy).then_inc(xt_hi_done, 1)

            def p_evac(n):
                act.wait_ge(p_done, n.count(1, 1))
                nc.scalar.activation(p_hi[:, :], p_bank[:, :], ACT.Copy).then_inc(p_hi_done, 1)

            def front(n):
                for k in MATRICES:
                    act.wait_ge(weights["ffn_loaded"][k], 16)
                    nc.scalar.activation(w[k][0][:, :], weights[k][:, :], ACT.Copy, scale=0.5 if k == "V2" else 1.0)\
                        .then_inc(w_rounded, 1)
                    if k == "U1":
                        for t in range(KD):
                            turn(n, t)
                p_evac(n)

            def step(n, ahead):
                for j in range(FT):
                    act.wait_ge(h_done, n.count(FT, j + 1))
                    if j >= RING:
                        act.wait_ge(h_lo_done, n.count(FT, j + 1 - RING))
                    nc.scalar.activation(h[:, j % RING], h_bank[j % RING][:, :], ACT.Gelu_apprx_tanh, bias=b1[:, j:j + 1])\
                        .then_inc(gelu_done, 1)
                    act.wait_ge(gelu_done, n.count(FT, j + 1))
                    if j >= RING:
                        act.wait_ge(h_used, n.count(FT, j + 1 - RING))
                    nc.scalar.activation(h_hi[:, j % RING], h[:, j % RING], ACT.Copy).then_inc(h_hi_done, 1)
                    if ahead and 0 <= j - TURN_AT - 1 < KD:
                        turn(n + 1, j - TURN_AT - 1)
                act.wait_ge(h_used, n.count(FT, FT))
                nc.scalar.activation(q_hi[:, :], q_bank[:, :], ACT.Copy).then_inc(q_hi_done, 1)
                if ahead:
                    p_evac(n + 1)

            steps(act, front, step)

        @block.vector
        def _(dve):
            def tile_stats(n, j):
                if j == 0:
                    dve.wait_ge(loaded[n.parity], (n.turn() + 1) * 16)
                nc.vector.bn_stats(stats[:, j], x_ld[:, n.parity, j]).then_inc(stats_raw, 1)

            def tile_moments(j):
                nc.vector.bn_aggr(mv[:, j], stats[:, j]).then_inc(stats_done, 1)

            def tile_norm(n, j):
                if j == 0:
                    dve.wait_ge(rstd_done, n.count(1, 1))
                    dve.wait_ge(turned, n.count(KD))
                nc.vector.tensor_scalar(xn[:, j], x_ld[:, n.parity, j], mv[:, j, 0:1], rstd[:, j:j + 1],
                                        ALU.subtract, ALU.mult).then_inc(xn_done, 1)

            def turn(n, k):
                dve.wait_ge(xt_hi_done, n.count(KD, k + 1))
                nc.vector.tensor_tensor(xt_lo[:, k], to_bank[k % 2][:, :], as_f32(xt_hi[:, k]), ALU.subtract)\
                    .then_inc(xt_lo_done, 1)

            def p_evac(n):
                dve.wait_ge(p_hi_done, n.count(1, 1))
                nc.vector.tensor_tensor(p_lo[:, :], p_bank[:, :], as_f32(p_hi[:, :]), ALU.subtract).then_inc(p_lo_done, 1)

            def front(n):
                for j in range(TILES):
                    tile_stats(n, j)
                    dve.wait_ge(stats_raw, j + 1)
                    tile_moments(j)
                for j in range(TILES):
                    tile_norm(n, j)
                for i, k in enumerate(MATRICES):
                    dve.wait_ge(w_rounded, i + 1)
                    nc.vector.scalar_tensor_tensor(w[k][1][:, :], weights[k][:, :], 0.5 if k == "V2" else 1.0,
                                                   as_f32(w[k][0][:, :]), ALU.mult, ALU.subtract).then_inc(w_split, 1)
                    if k == "U1":
                        for t in range(KD):
                            turn(n, t)
                p_evac(n)

            def step(n, ahead):
                for j in range(FT):
                    moments_of = j - STATS_AT - 1 if ahead and 0 <= j - STATS_AT - 1 < TILES else None
                    if moments_of is not None:
                        dve.wait_ge(stats_raw, (n + 1).count(TILES, moments_of + 1))
                    dve.wait_ge(h_hi_done, n.count(FT, j + 1))
                    nc.vector.tensor_tensor(h_lo[:, j % RING], h[:, j % RING], as_f32(h_hi[:, j % RING]), ALU.subtract)\
                        .then_inc(h_lo_done, 1)
                    if moments_of is not None:
                        tile_moments(moments_of)
                    if ahead and 0 <= j - STATS_AT < TILES:
                        tile_stats(n + 1, j - STATS_AT)
                    if ahead and 0 <= j - NORM_AT < TILES:
                        tile_norm(n + 1, j - NORM_AT)
                    if ahead and 0 <= j - TURN_AT - 1 < KD:
                        turn(n + 1, j - TURN_AT - 1)
                dve.wait_ge(q_hi_done, n.count(1, 1))
                nc.vector.tensor_tensor(q_lo[:, :], q_bank[:, :], as_f32(q_hi[:, :]), ALU.subtract).then_inc(q_lo_done, 1)
                if ahead:
                    p_evac(n + 1)
                dve.wait_ge(xb_done, n.count(TILES, TILES))
                dve.wait_ge(stored, n.count(16))
                for j in range(TILES):
                    dve.wait_ge(o_done, n.count(TILES, j + 1))
                    nc.vector.tensor_tensor(y_out[:, j], to_bank[j % 2][:, :], xb[:, n.parity, j], ALU.add)\
                        .then_inc(y_done, 1)

            steps(dve, front, step)

        @block.tensor
        def _(pe):
            def product(out, w_hi, w_lo, m_hi, m_lo, start, stop):
                nc.tensor.matmul(out, w_hi, m_hi, start=start, stop=False)
                nc.tensor.matmul(out, w_lo, m_hi, start=False, stop=False)
                return nc.tensor.matmul(out, w_hi, m_lo, start=False, stop=stop)

            def turn(n, k, first=False):
                if k == 0:
                    pe.wait_ge(xn_done, n.count(TILES, TILES))
                    if not first:
                        pe.wait_ge(y_done, (n + -1).count(TILES))
                if k >= 2:
                    pe.wait_ge(xt_lo_done, n.count(KD, k - 1))
                for j in range(TILES):
                    last = nc.tensor.transpose(to_bank[k % 2][:, j * P:(j + 1) * P], xn[:, j, k * P:(k + 1) * P], ident[:, :])
                last.then_inc(turned, 1)

            def p_product(n):
                pe.wait_ge(p_lo_done, n.count(1))
                for k in range(KD):
                    pe.wait_ge(xt_lo_done, n.count(KD, k + 1))
                    last = product(p_bank[:, :], u1_hi[:, k * P:(k + 1) * P], u1_lo[:, k * P:(k + 1) * P],
                                   xt_hi[:, k], xt_lo[:, k], k == 0, k == KD - 1)
                last.then_inc(p_done, 1)

            def h_product(n, j):
                if j == 0:
                    pe.wait_ge(p_lo_done, n.count(1, 1))
                if j >= RING:
                    pe.wait_ge(gelu_done, n.count(FT, j + 1 - RING))
                f = slice(j * P, (j + 1) * P)
                product(h_bank[j % RING][:, :], v1_hi[:, f], v1_lo[:, f], p_hi[:, :], p_lo[:, :], True, True)\
                    .then_inc(h_done, 1)

            def q_product(n, j):
                if j == 0:
                    pe.wait_ge(q_lo_done, n.count(1))
                pe.wait_ge(h_lo_done, n.count(FT, j + 1))
                r = slice(j * P, (j + 1) * P)
                last = product(q_bank[:, :], u2_hi[:, r], u2_lo[:, r], h_hi[:, j % RING], h_lo[:, j % RING],
                               j == 0, j == FT - 1)
                last.then_inc(h_used, 1)

            def o_product(n, ahead):
                pe.wait_ge(q_lo_done, n.count(1, 1))
                for j in range(TILES):
                    if j < 2 and ahead:
                        pe.wait_ge(xt_lo_done, (n + 1).count(KD, KD - 1 + j))
                    if j >= 2 or not ahead:
                        pe.wait_ge(y_done, n.count(TILES, j - 1))
                    t = slice(j * P, (j + 1) * P)
                    product(to_bank[j % 2][:, :], q_hi[:, t], q_lo[:, t], v2_hi[:, :], v2_lo[:, :], True, True)\
                        .then_inc(o_done, 1)

            def front(n):
                for k in range(KD):
                    turn(n, k, first=True)
                pe.wait_ge(w_split, 1)
                p_product(n)
                pe.wait_ge(w_split, len(MATRICES))

            def step(n, ahead):
                for j in range(FT + LAG):
                    if j < FT:
                        h_product(n, j)
                    if j >= LAG:
                        q_product(n, j - LAG)
                    if ahead and 0 <= j - TURN_AT < KD:
                        turn(n + 1, j - TURN_AT)
                if ahead:
                    p_product(n + 1)
                o_product(n, ahead)

            steps(pe, front, step)


def mlstm_phase(nc, x_in, x_out, seq, weights):
    T, D = x_in.shape
    H = 8
    DK, DV = 32, D // H
    DV1 = DV + 1
    C = P
    TOK = 2 * C
    KD = D // P
    G = 2
    HG = H // G
    NS = T // TOK
    GATES = 40
    ROWS = 72
    QK_SCALE = float(DK) ** -0.5
    assert seq == 4 * TOK and NS % 2 == 0 and NS >= 4 and D == 512

    src = x_in.rearrange("(n c p) d -> n p c d", p=P, c=2)
    dst = x_out.rearrange("(n c p) d -> n p c d", p=P, c=2)

    with ExitStack() as ctx:
        def sb(label, shape, dt=F32):
            return ctx.enter_context(nc.sbuf_tensor(f"cell_{label}", shape, dt))

        def sem(label):
            return ctx.enter_context(nc.semaphore(f"cell_{label}"))

        def psum(label, shape):
            return ctx.enter_context(nc.psum_tensor(f"cell_{label}", shape, F32))

        staged = weights["cell_staged"]
        sizes = {"qk": KD * 2 * G * P, "vo": KD * 2 * D, "gate": KD * GATES, "out": KD * D}
        w = {k: (sb(f"w_{k}_hi", [P, n], F32R), sb(f"w_{k}_lo", [P, n], F32R)) for k, n in sizes.items()}

        ogw = staged[:, 0:2048].rearrange("p (u c d) -> p u c d", u=2, c=2)
        ogb = staged[:, 2048:4096].rearrange("p (u c d) -> p u c d", u=2, c=2)
        wt = staged[:, 4096:6144].rearrange("p (g c n) -> p g c n", g=G, c=2)

        y_out = staged[:, 6144:7168].rearrange("p (c d) -> p c d", c=2)
        a = staged[:, 7168:8192].rearrange("p (g n) -> p g n", g=G)

        x_ln = sb("x_ln", [P, 2, 2, D])
        x_res = sb("x_res", [P, 2, D])
        xt_hi, xt_lo = sb("xt_hi", [P, KD, TOK], F32R), sb("xt_lo", [P, KD, TOK], F32R)
        stats, mv, veps, rstd = sb("stats", [P, 2, 6]), sb("mv", [P, 2, 2]), sb("veps", [P, 2]), sb("rstd", [P, 2])
        q_s = sb("q_s", [P, G, TOK])
        q_bd = sb("q_bd", [P, G, 2, HG, C])
        q_d = sb("q_d", [P, 2, G, TOK])
        k_t = sb("k_t", [P, 2, G, TOK])
        k_w = sb("k_w", [P, 2, 2, H * DK])
        v1 = sb("v1", [P, 2, 2, H, DV1])
        og = sb("og", [P, D])
        gate = sb("gate", [H, 2, TOK])
        m_run = sb("m_run", [H, TOK + 1])
        log_f, d_sum = sb("log_f", [H, TOK]), sb("d_sum", [H, TOK])
        zeros = sb("zeros", [H, C])
        rows = sb("rows", [96, TOK])
        d_split = sb("d_split", [GATES, 2, TOK], F32R)
        cols = sb("cols", [P, 2, 2, ROWS])
        e_m = sb("e_m", [P, 2, 2, H])
        e_last = sb("e_last", [P, 2, H])
        e_d = sb("e_d", [P, 2, G, TOK])
        state = sb("state", [P, G, DV1])
        state_bd = sb("state_bd", [P, G, HG, DV1])
        den, rden = sb("den", [P, G, HG]), sb("rden", [P, G, HG])
        h, ho = sb("h", [P, D]), sb("ho", [P, D])
        h_stats, h_mv, h_veps, h_rstd = sb("h_stats", [P, 6]), sb("h_mv", [P, 2]), sb("h_veps", [P, 1]), sb("h_rstd", [P, 1])
        hot_hi, hot_lo = sb("hot_hi", [P, KD, C], F32R), sb("hot_lo", [P, KD, C], F32R)
        keep_m, keep_c = sb("keep_m", [H, 1]), sb("keep_c", [P, 1])

        wb = [psum(f"wb{i}", [P, 512]) for i in range(2)]
        gb = psum("gb", [P, 512])
        d_bc = psum("d_bc", [P, HG, TOK])
        s_b = psum("s_b", [P, 512])
        n_b = psum("n_b", [P, G, 512])

        names = """w_rounded w_split made stats_raw stats_done veps_done rstd_done xn_done turned xt_hi_done xt_lo_done
            gates_done tanh_done chain keep_m_done rows_turned cols_done e_cols_done exp_d_mm e_d_done
            q_mm q_done k_mm k_done v_mm v_done og_mm og_tanh_done og_done ogw_done kt_mm k_w_done q_d_done
            d_bc_done e_done wt_done s_done a_done n_done den_step h_done c_mm c_done keep_c_done keep_c_turned bd_done
            h_stats_raw h_stats_done h_veps_done h_rstd_done h_norm_done h_scaled_done ho_done
            hot_mm hot_hi_done hot_lo_done y_mm y_done stored res_loaded q_bd_done"""
        S = {k: sem(k) for k in names.split()}
        ln_loaded = [sem("ln_loaded0"), sem("ln_loaded1")]
        CHAIN = 14
        MADE = 9

        sel_head, sel_part, mask, head_mask = (weights[k] for k in ("sel_head", "sel_part", "mask", "head_mask"))
        ident, minus_half = weights["ident"], weights["minus_half"]
        offsets = {"qk": 0, "vo": sizes["qk"], "gate": sizes["qk"] + sizes["vo"]}
        offsets["out"] = offsets["gate"] + sizes["gate"]

        block = ctx.enter_context(nc.Block())

        def steps(eng, front, step):
            front(At(0, 0))
            step(At(0, 0), True, True)
            with eng.Fori(0, NS // 2 - 2) as pair:
                for u in (1, 2):
                    step(At(pair, u), True, True)
            step(At(0, NS - 3), True, True)
            step(At(0, NS - 2), True, False)
            step(At(0, NS - 1), False, False)

        @block.sync
        def _(sp):
            def part(n, view):
                return view[bass.ds(n.pair * 2 + n.offset, 1)].rearrange("a p c d -> (a p) c d")

            def load_ln(n):
                sp.dma_start(x_ln[:, n.parity], part(n, src)).then_inc(ln_loaded[n.parity], 16)

            def load_res(n):
                sp.dma_start(x_res[:, :, :], part(n, src)).then_inc(S["res_loaded"], 16)

            def step(n, res, ln):
                if ln:
                    sp.wait_ge(S["turned"], (n + 1).count(2, 2))
                    load_ln(n + 3)
                sp.wait_ge(S["y_done"], n.count(2, 2))
                sp.dma_start(part(n, dst), y_out[:, :, :]).then_inc(S["stored"], 16)
                if res:
                    load_res(n + 1)

            for n in range(2):
                load_ln(At(0, n))
            load_res(At(0, 0))
            sp.wait_ge(S["turned"], 2)
            load_ln(At(0, 2))
            with sp.Fori(0, NS // 2 - 2) as pair:
                for u in range(2):
                    step(At(pair, u), True, True)
            for n in range(NS - 4, NS):
                step(At(0, n), n + 1 < NS, n + 3 < NS)
            sp.wait_ge(S["stored"], 16 * NS)

        @block.gpsimd
        def _(pool):
            nc.gpsimd.memset(state[:, :, :], 0.0).then_inc(S["made"], 1)
            nc.gpsimd.memset(state_bd[:, :, :, :], 0.0).then_inc(S["made"], 1)
            nc.gpsimd.memset(v1[:, :, :, :, :], 1.0).then_inc(S["made"], 1)
            nc.gpsimd.memset(rows[:, :], 0.0).then_inc(S["made"], 1)
            nc.gpsimd.memset(as_f32(d_split[:, :, :]), 0.0).then_inc(S["made"], 1)
            nc.gpsimd.memset(zeros[:, :], 0.0).then_inc(S["made"], 1)
            nc.gpsimd.memset(m_run[:, :], 0.0).then_inc(S["made"], 1)
            nc.gpsimd.memset(keep_m[:, :], 0.0).then_inc(S["made"], 1)
            nc.gpsimd.memset(keep_c[:, :], 0.0).then_inc(S["made"], 1)

            def x_rstd(n):
                pool.wait_ge(S["stats_done"], n.count(2, 2))
                nc.gpsimd.tensor_tensor(veps[:, :], mv[:, :, 1], weights["ln_eps"][:, 0:2], ALU.add).then_inc(S["veps_done"], 1)
                pool.wait_ge(S["veps_done"], n.count(1, 1))
                nc.gpsimd.tensor_tensor(rstd[:, :], veps[:, :], minus_half[:, 0:2], ALU.pow).then_inc(S["rstd_done"], 1)

            def out_gate(n, c):
                pool.wait_ge(S["og_done"], n.count(2, c + 1))
                nc.gpsimd.tensor_tensor(ogw[:, n.parity, c], og[:, :], weights["ln_w"][:, :], ALU.mult).then_inc(S["ogw_done"], 1)
                nc.gpsimd.tensor_tensor(ogb[:, n.parity, c], og[:, :], weights["ln_b"][:, :], ALU.mult).then_inc(S["ogw_done"], 1)

            def spread(n, c):
                if c == 1 and n.parity == 1:
                    pool.wait_ge(S["keep_c_done"], n.turn() + 1)
                for g in range(G):
                    pool.wait_ge(S["c_done"], n.count(4, 2 * c + g + 1))
                    nc.gpsimd.tensor_tensor(state_bd[:, g], state[:, g].unsqueeze(1).broadcast_to([P, HG, DV1]),
                                            head_mask[:, :].unsqueeze(2).broadcast_to([P, HG, DV1]), ALU.mult)\
                        .then_inc(S["bd_done"], 1)

            def h_rstd_of(n, c):
                pool.wait_ge(S["h_stats_done"], n.count(2, c + 1))
                nc.gpsimd.tensor_tensor(h_veps[:, :], h_mv[:, 1:2], weights["cell_eps"][:, 0:1], ALU.add).then_inc(S["h_veps_done"], 1)
                pool.wait_ge(S["h_veps_done"], n.count(2, c + 1))
                nc.gpsimd.tensor_tensor(h_rstd[:, :], h_veps[:, :], minus_half[:, 0:1], ALU.pow).then_inc(S["h_rstd_done"], 1)

            def front(n):
                x_rstd(At(0, 0))
                x_rstd(At(0, 1))
                pool.wait_ge(S["w_split"], 4)
                out_gate(n, 0)
                out_gate(n, 1)

            def step(n, ahead, ln_ahead):
                if ln_ahead:
                    x_rstd(n + 2)
                spread(n, 0)
                h_rstd_of(n, 0)
                if ahead:
                    out_gate(n + 1, 0)
                spread(n, 1)
                h_rstd_of(n, 1)
                if ahead:
                    out_gate(n + 1, 1)

            steps(pool, front, step)

        @block.scalar
        def _(act):
            for k in ("gate", "qk", "vo", "out"):
                act.wait_ge(weights["cell_loaded"][k], 16)
                nc.scalar.activation(w[k][0][:, :], staged[:, offsets[k]:offsets[k] + sizes[k]], ACT.Copy)\
                    .then_inc(S["w_rounded"], 1)

            def turn(n):
                for b in range(2):
                    act.wait_ge(S["turned"], n.count(2, b + 1))
                    nc.scalar.activation(xt_hi[:, 2 * b:2 * b + 2], wb[b][:, :], ACT.Copy).then_inc(S["xt_hi_done"], 1)

            def gate_tanh(n):
                act.wait_ge(S["gates_done"], n.count(1, 1))
                act.wait_ge(S["chain"], n.count(CHAIN))
                for i, r in enumerate((0, 32)):
                    nc.scalar.activation(gate[:, i], gb[r:r + H, 0:TOK], ACT.Tanh, bias=weights["gate_bias"][r:r + H, :],
                                         scale=1.0 / CAP).then_inc(S["tanh_done"], 1)

            def q_evac(n):
                act.wait_ge(S["q_mm"], n.count(1, 1))
                nc.scalar.activation(q_s[:, :], wb[0][:, :], ACT.Copy, scale=QK_SCALE).then_inc(S["q_done"], 1)

            def q_spread(n):
                act.wait_ge(S["q_done"], n.count(1, 1))
                act.wait_ge(S["s_done"], n.count(4))
                for j in range(HG):
                    nc.scalar.activation(q_bd[:, :, :, j], q_s[:, :, :].rearrange("p g (c t) -> p g c t", c=2), ACT.Copy,
                                         scale=head_mask[:, j:j + 1]).then_inc(S["q_bd_done"], 1)

            def k_evac(n):
                act.wait_ge(S["k_mm"], n.count(1, 1))
                nc.scalar.activation(k_t[:, n.parity], wb[1][:, :], ACT.Copy).then_inc(S["k_done"], 1)

            def v_evac(n, c):
                act.wait_ge(S["v_mm"], n.count(2, c + 1))
                nc.scalar.activation(v1[:, n.parity, c, :, 0:DV], wb[c][:, :].rearrange("p (h e) -> p h e", e=DV), ACT.Copy)\
                    .then_inc(S["v_done"], 1)

            def og_evac(n, c):
                act.wait_ge(S["og_mm"], n.count(2, c + 1))
                act.wait_ge(S["ogw_done"], n.count(4, 2 * c))
                nc.scalar.activation(og[:, :], wb[1 - c][:, :], ACT.Tanh, scale=0.5).then_inc(S["og_tanh_done"], 1)
                act.wait_ge(S["og_tanh_done"], n.count(2, c + 1))
                nc.scalar.activation(og[:, :], og[:, :], ACT.Copy, scale=0.5, bias=0.5).then_inc(S["og_done"], 1)

            def e_cols(n):
                act.wait_ge(S["cols_done"], n.count(1, 1))
                nc.scalar.activation(e_last[:, :, :], cols[:, n.parity, :, 64:72], ACT.Exp).then_inc(S["e_cols_done"], 1)
                nc.scalar.activation(e_m[:, n.parity], cols[:, n.parity, :, 32:40], ACT.Exp, scale=-1.0).then_inc(S["e_cols_done"], 1)

            def e_d_evac(n):
                act.wait_ge(S["exp_d_mm"], n.count(1, 1))
                nc.scalar.activation(e_d[:, n.parity], wb[0][:, :], ACT.Exp).then_inc(S["e_d_done"], 1)

            def decay_weights(n, g):
                act.wait_ge(S["e_done"], n.count(4, 2 * g + 2))
                nc.scalar.activation(wt[:, g], wt[:, g], ACT.Exp).then_inc(S["wt_done"], 1)

            def hot_evac(n, c):
                act.wait_ge(S["hot_mm"], n.count(2, c + 1))
                nc.scalar.activation(hot_hi[:, :, :], wb[c][:, :], ACT.Copy).then_inc(S["hot_hi_done"], 1)

            def front(n):
                act.wait_ge(S["made"], MADE)
                turn(n)
                gate_tanh(n)
                q_evac(n)
                k_evac(n)
                v_evac(n, 0)
                e_cols(n)
                og_evac(n, 0)
                e_d_evac(n)
                q_spread(n)
                v_evac(n, 1)
                og_evac(n, 1)

            def step(n, ahead, ln_ahead):
                decay_weights(n, 0)
                if ahead:
                    turn(n + 1)
                    gate_tanh(n + 1)
                decay_weights(n, 1)
                if ahead:
                    q_evac(n + 1)
                    k_evac(n + 1)
                    v_evac(n + 1, 0)
                    e_cols(n + 1)
                    og_evac(n + 1, 0)
                    e_d_evac(n + 1)
                hot_evac(n, 0)
                if ahead:
                    q_spread(n + 1)
                    v_evac(n + 1, 1)
                hot_evac(n, 1)
                if ahead:
                    og_evac(n + 1, 1)

            steps(act, front, step)

        @block.vector
        def _(dve):
            def x_stats(n):
                dve.wait_ge(ln_loaded[n.parity], (n.turn() + 1) * 16)
                for j in range(2):
                    nc.vector.bn_stats(stats[:, j], x_ln[:, n.parity, j]).then_inc(S["stats_raw"], 1)
                dve.wait_ge(S["stats_raw"], n.count(2, 2))

            def x_moments(n):
                for j in range(2):
                    nc.vector.bn_aggr(mv[:, j], stats[:, j]).then_inc(S["stats_done"], 1)

            def x_norm(n):
                dve.wait_ge(S["rstd_done"], n.count(1, 1))
                for j in range(2):
                    nc.vector.tensor_scalar(x_ln[:, n.parity, j], x_ln[:, n.parity, j], mv[:, j, 0:1], rstd[:, j:j + 1],
                                            ALU.subtract, ALU.mult).then_inc(S["xn_done"], 1)

            def turn(n):
                for b in range(2):
                    dve.wait_ge(S["xt_hi_done"], n.count(2, b + 1))
                    ks = slice(2 * b, 2 * b + 2)
                    nc.vector.tensor_tensor(xt_lo[:, ks], wb[b][:, :], as_f32(xt_hi[:, ks]), ALU.subtract)\
                        .then_inc(S["xt_lo_done"], 1)

            def gate_chain(n):
                links = [0]

                def link(ins):
                    links[0] += 1
                    ins.then_inc(S["chain"], 1)
                    dve.wait_ge(S["chain"], n.count(CHAIN, links[0]))

                f, i, m, m_prev = gate[:, 0], gate[:, 1], m_run[:, 1:TOK + 1], m_run[:, 0:TOK]
                dve.wait_ge(S["tanh_done"], n.count(2, 2))
                link(nc.vector.tensor_scalar(gate[:, :, :], gate[:, :, :], CAP, None, ALU.mult))
                if n.parity == 0:
                    link(nc.vector.tensor_scalar(m_run[:, 0:1], m_run[:, TOK:TOK + 1], keep_m[:, 0:1], None, ALU.mult))
                    nc.vector.tensor_scalar(keep_m[:, :], keep_m[:, :], -1.0, 1.0, ALU.mult, ALU.add).then_inc(S["keep_m_done"], 1)
                    dve.wait_ge(S["keep_m_done"], n.turn() + 1)
                else:
                    link(nc.vector.tensor_copy(m_run[:, 0:1], m_run[:, TOK:TOK + 1]))
                link(nc.vector.tensor_tensor_scan(m, f, i, m_run[:, 0:1], ALU.add, ALU.max))
                link(nc.vector.tensor_tensor(log_f[:, :], f, m_prev, ALU.add))
                link(nc.vector.tensor_tensor(log_f[:, :], log_f[:, :], m, ALU.subtract))
                link(nc.vector.tensor_tensor(i, i, m, ALU.subtract))
                for c in range(2):
                    t = slice(c * C, (c + 1) * C)
                    link(nc.vector.tensor_tensor_scan(d_sum[:, t], log_f[:, t], zeros[:, :], 0.0, ALU.add, ALU.add))
                link(nc.vector.tensor_tensor(rows[0:H, :], i, d_sum[:, :], ALU.subtract))
                link(nc.vector.tensor_copy(rows[32:32 + H, :], m))
                for c in range(2):
                    t = slice(c * C, (c + 1) * C)
                    last = (c + 1) * C - 1
                    link(nc.vector.tensor_scalar(rows[64:64 + H, t], rows[0:H, t], d_sum[:, last:last + 1], None, ALU.add))
                link(nc.vector.tensor_copy(d_split[0:H, n.parity], d_sum[:, :]))
                link(nc.vector.tensor_tensor(d_split[32:32 + H, n.parity], d_sum[:, :], as_f32(d_split[0:H, n.parity]), ALU.subtract))
                assert links[0] == CHAIN

            def cols_evac(n):
                dve.wait_ge(S["rows_turned"], n.count(1, 1))
                nc.vector.tensor_copy(cols[:, n.parity], gb[:, 256:256 + 2 * ROWS].rearrange("p (c r) -> p c r", c=2))\
                    .then_inc(S["cols_done"], 1)

            def k_weighted(n):
                dve.wait_ge(S["kt_mm"], n.count(1, 1))
                dve.wait_ge(S["e_cols_done"], n.count(2, 1))
                for c in range(2):
                    nc.vector.tensor_tensor(k_w[:, n.parity, c].rearrange("p (h e) -> p h e", e=DK),
                                            wb[0][:, c * 256:(c + 1) * 256].rearrange("p (h e) -> p h e", e=DK),
                                            e_last[:, c].unsqueeze(2).broadcast_to([P, H, DK]), ALU.mult)\
                        .then_inc(S["k_w_done"], 1)

            def q_decayed(n):
                dve.wait_ge(S["e_d_done"], n.count(1, 1))
                dve.wait_ge(S["q_done"], n.count(1, 1))
                nc.vector.tensor_tensor(q_d[:, n.parity], q_s[:, :], e_d[:, n.parity], ALU.mult).then_inc(S["q_d_done"], 1)

            def exponents(n, g):
                dve.wait_ge(S["d_bc_done"], n.count(2, g + 1))
                dve.wait_ge(S["cols_done"], n.count(1, 1))
                for c in range(2):
                    for j in range(HG):
                        r = g * HG + j
                        last = nc.vector.scalar_tensor_tensor(wt[:, g, c, j * C:(j + 1) * C], d_bc[:, j, c * C:(c + 1) * C],
                                                              cols[:, n.parity, c, r:r + 1], mask[:, :], ALU.add, ALU.min)
                    last.then_inc(S["e_done"], 1)

            def attend(n, c, g):
                dve.wait_ge(S["wt_done"], n.count(2, g + 1))
                dve.wait_ge(S["s_done"], n.count(4, 2 * c + g + 1))
                nc.vector.tensor_tensor(a[:, g], s_b[:, :], wt[:, g, c], ALU.mult).then_inc(S["a_done"], 1)

            def normalise(n, c):
                dve.wait_ge(S["n_done"], n.count(2, c + 1))
                dve.wait_ge(S["e_cols_done"], n.count(2, 2))
                num = n_b[:, :, 0:HG * DV1].rearrange("p g (h e) -> p g h e", e=DV1)
                qn = num[:, :, :, DV]
                nc.vector.scalar_tensor_tensor(den[:, :, :], qn, -1.0, e_m[:, n.parity, c].rearrange("p (g h) -> p g h", g=G),
                                               ALU.mult, ALU.max).then_inc(S["den_step"], 1)
                dve.wait_ge(S["den_step"], n.count(8, 4 * c + 1))
                nc.vector.tensor_tensor(den[:, :, :], qn, den[:, :, :], ALU.max).then_inc(S["den_step"], 1)
                dve.wait_ge(S["den_step"], n.count(8, 4 * c + 2))
                nc.vector.tensor_scalar(den[:, :, :], den[:, :, :], CELL_EPS, None, ALU.add).then_inc(S["den_step"], 1)
                dve.wait_ge(S["den_step"], n.count(8, 4 * c + 3))
                nc.vector.reciprocal(rden[:, :, :], den[:, :, :]).then_inc(S["den_step"], 1)
                dve.wait_ge(S["den_step"], n.count(8, 4 * c + 4))
                nc.vector.tensor_tensor(h[:, :].rearrange("p (g h e) -> p g h e", g=G, e=DV), num[:, :, :, 0:DV],
                                        rden[:, :, :].unsqueeze(3).broadcast_to([P, G, HG, DV]), ALU.mult)\
                    .then_inc(S["h_done"], 1)

            def update_state(n, c):
                dve.wait_ge(S["c_mm"], n.count(2, c + 1))
                for g in range(G):
                    last = (c + 1) * C - 1
                    nc.vector.scalar_tensor_tensor(state[:, g], state[:, g], e_d[:, n.parity, g, last:last + 1],
                                                   wb[1][:, g * DV1:(g + 1) * DV1], ALU.mult, ALU.add).then_inc(S["c_done"], 1)
                if c == 1 and n.parity == 1:
                    dve.wait_ge(S["c_done"], n.count(4, 4))
                    nc.vector.tensor_scalar(keep_c[:, :], keep_c[:, :], -1.0, 1.0, ALU.mult, ALU.add).then_inc(S["keep_c_turned"], 1)
                    dve.wait_ge(S["keep_c_turned"], n.turn() + 1)
                    nc.vector.tensor_scalar(state[:, :, :], state[:, :, :], keep_c[:, 0:1], None, ALU.mult).then_inc(S["keep_c_done"], 1)

            def h_statistics(n, c):
                dve.wait_ge(S["h_done"], n.count(2, c + 1))
                nc.vector.bn_stats(h_stats[:, :], h[:, :]).then_inc(S["h_stats_raw"], 1)
                dve.wait_ge(S["h_stats_raw"], n.count(2, c + 1))

            def h_moments():
                nc.vector.bn_aggr(h_mv[:, :], h_stats[:, :]).then_inc(S["h_stats_done"], 1)

            def gated(n, c):
                dve.wait_ge(S["h_rstd_done"], n.count(2, c + 1))
                nc.vector.tensor_scalar(h[:, :], h[:, :], h_mv[:, 0:1], h_rstd[:, 0:1], ALU.subtract, ALU.mult)\
                    .then_inc(S["h_norm_done"], 1)
                dve.wait_ge(S["h_norm_done"], n.count(2, c + 1))
                dve.wait_ge(S["ogw_done"], n.count(4, 2 * c + 2))
                nc.vector.tensor_tensor(h[:, :], h[:, :], ogw[:, n.parity, c], ALU.mult).then_inc(S["h_scaled_done"], 1)
                dve.wait_ge(S["h_scaled_done"], n.count(2, c + 1))
                nc.vector.tensor_tensor(ho[:, :], h[:, :], ogb[:, n.parity, c], ALU.add).then_inc(S["ho_done"], 1)

            def hot_evac(n, c):
                dve.wait_ge(S["hot_hi_done"], n.count(2, c + 1))
                nc.vector.tensor_tensor(hot_lo[:, :, :], wb[c][:, :], as_f32(hot_hi[:, :, :]), ALU.subtract)\
                    .then_inc(S["hot_lo_done"], 1)

            def residual(n, c):
                if c == 0:
                    dve.wait_ge(S["res_loaded"], n.count(16, 16))
                    dve.wait_ge(S["stored"], n.count(16))
                dve.wait_ge(S["y_mm"], n.count(2, c + 1))
                nc.vector.tensor_tensor(y_out[:, c], wb[c][:, :], x_res[:, c], ALU.add).then_inc(S["y_done"], 1)

            def front(n):
                x_stats(At(0, 0))
                x_moments(At(0, 0))
                x_norm(At(0, 0))
                x_stats(At(0, 1))
                x_moments(At(0, 1))
                for i, k in enumerate(("gate", "qk", "vo", "out")):
                    dve.wait_ge(S["w_rounded"], i + 1)
                    nc.vector.tensor_tensor(w[k][1][:, :], staged[:, offsets[k]:offsets[k] + sizes[k]], as_f32(w[k][0][:, :]),
                                            ALU.subtract).then_inc(S["w_split"], 1)
                    if k == "gate":
                        turn(n)
                        dve.wait_ge(S["made"], MADE)
                        gate_chain(n)
                        x_norm(At(0, 1))
                cols_evac(n)
                k_weighted(n)
                q_decayed(n)

            def step(n, ahead, ln_ahead):
                exponents(n, 0)
                if ahead:
                    turn(n + 1)
                exponents(n, 1)
                attend(n, 0, 0)
                if ahead:
                    gate_chain(n + 1)
                attend(n, 0, 1)
                if ln_ahead:
                    x_stats(n + 2)
                normalise(n, 0)
                if ln_ahead:
                    x_moments(n + 2)
                update_state(n, 0)
                if ahead:
                    cols_evac(n + 1)
                h_statistics(n, 0)
                if ahead:
                    k_weighted(n + 1)
                h_moments()
                attend(n, 1, 0)
                if ln_ahead:
                    x_norm(n + 2)
                gated(n, 0)
                attend(n, 1, 1)
                normalise(n, 1)
                update_state(n, 1)
                h_statistics(n, 1)
                hot_evac(n, 0)
                h_moments()
                gated(n, 1)
                residual(n, 0)
                if ahead:
                    q_decayed(n + 1)
                hot_evac(n, 1)
                residual(n, 1)

            steps(dve, front, step)

        @block.tensor
        def _(pe):
            def product(out, pairs):
                for i, (w_hi, w_lo, m_hi, m_lo) in enumerate(pairs):
                    nc.tensor.matmul(out, w_hi, m_hi, start=(i == 0), stop=False)
                    nc.tensor.matmul(out, w_lo, m_hi, start=False, stop=False)
                    last = nc.tensor.matmul(out, w_hi, m_lo, start=False, stop=(i == len(pairs) - 1))
                return last

            def turn(n, first=False):
                pe.wait_ge(S["xn_done"], n.count(2, 2))
                for b in range(2):
                    if not first:
                        if b == 0:
                            pe.wait_ge(S["og_tanh_done"], n.count(2))
                        else:
                            pe.wait_ge(S["y_done"], (n + -1).count(2))
                    for k in (2 * b, 2 * b + 1):
                        for j in range(2):
                            last = nc.tensor.transpose(wb[b][:, (k % 2) * TOK + j * P:(k % 2) * TOK + (j + 1) * P],
                                                       x_ln[:, n.parity, j, k * P:(k + 1) * P], ident[:, :])
                    last.then_inc(S["turned"], 1)

            def gates(n):
                pe.wait_ge(S["xt_lo_done"], n.count(2, 2))
                pe.wait_ge(S["cols_done"], n.count(1))
                cols_of = [slice(k * GATES, (k + 1) * GATES) for k in range(KD)]
                product(gb[0:GATES, 0:TOK], [(w["gate"][0][:, s], w["gate"][1][:, s], xt_hi[:, k], xt_lo[:, k])
                                             for k, s in enumerate(cols_of)]).then_inc(S["gates_done"], 1)

            def qk_part(bank, n, base):
                for g in range(G):
                    at = [slice(k * 2 * G * P + base + g * P, k * 2 * G * P + base + (g + 1) * P) for k in range(KD)]
                    last = product(bank[:, g * TOK:(g + 1) * TOK],
                                   [(w["qk"][0][:, s], w["qk"][1][:, s], xt_hi[:, k], xt_lo[:, k]) for k, s in enumerate(at)])
                return last

            def q_proj(n):
                qk_part(wb[0], n, 0).then_inc(S["q_mm"], 1)

            def k_proj(n):
                qk_part(wb[1], n, G * P).then_inc(S["k_mm"], 1)

            def vo_part(bank, c, base):
                t = slice(c * C, (c + 1) * C)
                at = [slice(k * 2 * D + base, k * 2 * D + base + D) for k in range(KD)]
                return product(bank[:, :], [(xt_hi[:, k, t], xt_lo[:, k, t], w["vo"][0][:, s], w["vo"][1][:, s])
                                            for k, s in enumerate(at)])

            def v_proj(n, c):
                vo_part(wb[c], c, 0).then_inc(S["v_mm"], 1)

            def og_proj(n, c):
                vo_part(wb[1 - c], c, D).then_inc(S["og_mm"], 1)

            def turn_rows(n):
                pe.wait_ge(S["chain"], n.count(CHAIN, CHAIN))
                for c in range(2):
                    last = nc.tensor.transpose(gb[:, 256 + c * ROWS:256 + (c + 1) * ROWS], rows[0:ROWS, c * C:(c + 1) * C],
                                               ident[0:ROWS, 0:ROWS])
                last.then_inc(S["rows_turned"], 1)

            def turn_k(n):
                pe.wait_ge(S["k_done"], n.count(1, 1))
                pe.wait_ge(S["v_done"], n.count(2, 1))
                for c in range(2):
                    for g in range(G):
                        last = nc.tensor.transpose(wb[0][:, c * 256 + g * P:c * 256 + (g + 1) * P],
                                                   k_t[:, n.parity, g, c * C:(c + 1) * C], ident[:, :])
                last.then_inc(S["kt_mm"], 1)

            def spread_d(n):
                pe.wait_ge(S["k_w_done"], n.count(2, 2))
                for g in range(G):
                    last = nc.tensor.matmul(wb[0][:, g * TOK:(g + 1) * TOK], sel_part[:, g * P:(g + 1) * P],
                                            d_split[:, n.parity], start=True, stop=True)
                last.then_inc(S["exp_d_mm"], 1)

            def broadcast_d(n, g):
                pe.wait_ge(S["e_done"], n.count(4, 2 * g))
                for j in range(HG):
                    r = g * HG + j
                    last = nc.tensor.matmul(d_bc[:, j], sel_head[:, r * P:(r + 1) * P], d_split[:, n.parity], start=True, stop=True)
                last.then_inc(S["d_bc_done"], 1)

            def scores(n, c, g):
                pe.wait_ge(S["a_done"], n.count(4, 2 * c + g))
                pe.wait_ge(S["q_bd_done"], n.count(HG, HG))
                last = nc.tensor.matmul(s_b[:, :], k_t[:, n.parity, g, c * C:(c + 1) * C],
                                        q_bd[:, g, c].rearrange("p h t -> p (h t)"), start=True, stop=True)
                last.then_inc(S["s_done"], 1)

            def numerator(n, c):
                pe.wait_ge(S["h_done"], n.count(2, c))
                pe.wait_ge(S["q_d_done"], n.count(1, 1))
                for g in range(G):
                    pe.wait_ge(S["bd_done"], n.count(4, 2 * c))
                    nc.tensor.matmul(n_b[:, g, 0:HG * DV1], q_d[:, n.parity, g, c * C:(c + 1) * C],
                                     state_bd[:, g].rearrange("p h e -> p (h e)"), start=True, stop=False)
                    pe.wait_ge(S["a_done"], n.count(4, 2 * c + g + 1))
                    for j in range(HG):
                        last = nc.tensor.matmul(n_b[:, g, j * DV1:(j + 1) * DV1], a[:, g, j * C:(j + 1) * C],
                                                v1[:, n.parity, c, g * HG + j], start=False, stop=(j == HG - 1))
                last.then_inc(S["n_done"], 1)

            def state_product(n, c):
                for g in range(G):
                    for j in range(HG):
                        r = g * HG + j
                        last = nc.tensor.matmul(wb[1][j * DK:(j + 1) * DK, g * DV1:(g + 1) * DV1],
                                                k_w[:, n.parity, c, r * DK:(r + 1) * DK], v1[:, n.parity, c, r],
                                                start=True, stop=True)
                last.then_inc(S["c_mm"], 1)

            def turn_h(n, c):
                pe.wait_ge(S["ho_done"], n.count(2, c + 1))
                for k in range(KD):
                    last = nc.tensor.transpose(wb[c][:, k * P:(k + 1) * P], ho[:, k * P:(k + 1) * P], ident[:, :])
                last.then_inc(S["hot_mm"], 1)

            def out_proj(n, c):
                pe.wait_ge(S["hot_lo_done"], n.count(2, c + 1))
                product(wb[c][:, :], [(hot_hi[:, k], hot_lo[:, k], w["out"][0][:, k * D:(k + 1) * D], w["out"][1][:, k * D:(k + 1) * D])
                                      for k in range(KD)]).then_inc(S["y_mm"], 1)

            def front(n):
                turn(n, first=True)
                pe.wait_ge(S["w_split"], 1)
                gates(n)
                pe.wait_ge(S["w_split"], 3)
                q_proj(n)
                k_proj(n)
                pe.wait_ge(S["q_done"], n.count(1, 1))
                v_proj(n, 0)
                turn_rows(n)
                turn_k(n)
                og_proj(n, 0)
                spread_d(n)
                pe.wait_ge(S["og_tanh_done"], n.count(2, 1))
                v_proj(n, 1)
                pe.wait_ge(S["e_d_done"], n.count(1, 1))
                og_proj(n, 1)
                pe.wait_ge(S["w_split"], 4)

            def step(n, ahead, ln_ahead):
                f = n + 1
                broadcast_d(n, 0)
                if ahead:
                    turn(f)
                    gates(f)
                broadcast_d(n, 1)
                if ahead:
                    q_proj(f)
                scores(n, 0, 0)
                if ahead:
                    k_proj(f)
                scores(n, 0, 1)
                if ahead:
                    pe.wait_ge(S["q_done"], f.count(1, 1))
                    v_proj(f, 0)
                numerator(n, 0)
                if ahead:
                    pe.wait_ge(S["k_done"], f.count(1, 1))
                else:
                    pe.wait_ge(S["y_done"], n.count(2))
                state_product(n, 0)
                if ahead:
                    turn_rows(f)
                    turn_k(f)
                    pe.wait_ge(S["c_done"], n.count(4, 2))
                    og_proj(f, 0)
                scores(n, 1, 0)
                if ahead:
                    spread_d(f)
                scores(n, 1, 1)
                numerator(n, 1)
                if ahead:
                    pe.wait_ge(S["og_tanh_done"], f.count(2, 1))
                else:
                    pe.wait_ge(S["c_done"], n.count(4, 2))
                state_product(n, 1)
                if ahead:
                    pe.wait_ge(S["e_d_done"], f.count(1, 1))
                else:
                    pe.wait_ge(S["og_tanh_done"], n.count(2, 2))
                turn_h(n, 0)
                pe.wait_ge(S["c_done"], n.count(4, 4))
                if ahead:
                    v_proj(f, 1)
                out_proj(n, 0)
                if ahead:
                    pe.wait_ge(S["v_done"], f.count(2, 2))
                turn_h(n, 1)
                if ahead:
                    pe.wait_ge(S["y_done"], n.count(2, 1))
                    og_proj(f, 1)
                out_proj(n, 1)

            steps(pe, front, step)


def macaron_kernel(nc, x, wqk, wvo, wgate, wout, gate_bias, ln_w, ln_b, u1, v1, b1, u2, v2, b2,
                   ident, mask, sel_head, sel_part, head_mask, out):
    Bs, seq, D = x.shape
    x0 = x.rearrange("b s d -> (b s) d")
    y = out.rearrange("b s d -> (b s) d")
    x1 = nc.dram_tensor("x_after_ffn1", [Bs * seq, D], F32, kind="Internal").ap()
    x2 = nc.dram_tensor("x_after_cell", [Bs * seq, D], F32, kind="Internal").ap()

    with ExitStack() as ctx:
        def sb(label, shape, dt=F32):
            return ctx.enter_context(nc.sbuf_tensor(label, shape, dt))

        def sem(label):
            return ctx.enter_context(nc.semaphore(label))

        ffn_parts = {"U1": u1, "V1": v1, "U2": u2, "V2": v2}
        cell_parts = {"gate": wgate, "qk": wqk, "vo": wvo, "out": wout}
        order = ("qk", "vo", "gate", "out")
        weights = {k: sb(f"staged_{k}", [P, d.shape[1]]) for k, d in ffn_parts.items()}
        cell_staged = sb("cell_staged", [P, sum(cell_parts[k].shape[1] for k in order)])
        weights["cell_staged"] = cell_staged
        rows = {"ident": (ident, [P, P]), "mask": (mask, [P, P]), "head_mask": (head_mask, [P, 4]), "b1": (b1, [P, b1.shape[1]]),
                "ln_w": (ln_w, [P, D]), "ln_b": (ln_b, [P, D])}
        for k, (_, shape) in rows.items():
            weights[k] = sb(f"w_{k}", shape)
        weights["b2_half"] = sb("b2_half", [P, D])
        filled = {"minus_half": -0.5, "ln_eps": LN_EPS, "cell_eps": CELL_EPS}
        for k in filled:
            weights[k] = sb(k, [P, 4])
        weights["gate_bias"] = sb("w_gate_bias", [40, 1])
        sels = {"sel_head": sel_head, "sel_part": sel_part}
        for k, d in sels.items():
            weights[k] = sb(f"w_{k}", [40, d.shape[1]], F32R)

        small_loaded, sel_rounded, scaled = sem("small_loaded"), sem("sel_rounded"), sem("scaled")
        weights["ffn_loaded"] = {k: sem(f"loaded_{k}") for k in ffn_parts}
        weights["cell_loaded"] = {k: sem(f"loaded_{k}") for k in cell_parts}

        with ExitStack() as setup:
            b2_row = setup.enter_context(nc.sbuf_tensor("b2_row", [P, D], F32))
            bias_raw = setup.enter_context(nc.sbuf_tensor("bias_raw", [40, 1], F32))
            sel_raw = {k: setup.enter_context(nc.sbuf_tensor(f"raw_{k}", [40, d.shape[1]], F32)) for k, d in sels.items()}
            SMALL = len(rows) + 4
            with nc.Block() as block:
                @block.sync
                def _(sp):
                    for k, (d, _) in rows.items():
                        d = d.partition_broadcast(P) if len(d.shape) == 1 else d
                        sp.dma_start(weights[k][:, :], d).then_inc(small_loaded, 16)
                    sp.dma_start(b2_row[:, :], b2.partition_broadcast(P)).then_inc(small_loaded, 16)
                    sp.dma_start(bias_raw[:, :], gate_bias).then_inc(small_loaded, 16)
                    for k, d in sels.items():
                        sp.dma_start(sel_raw[k][:, :], d).then_inc(small_loaded, 16)
                    for k, d in ffn_parts.items():
                        sp.dma_start(weights[k][:, :], d).then_inc(weights["ffn_loaded"][k], 16)
                    at = 0
                    for k in order:
                        n = cell_parts[k].shape[1]
                        sp.dma_start(cell_staged[:, at:at + n], cell_parts[k]).then_inc(weights["cell_loaded"][k], 16)
                        at += n

                @block.gpsimd
                def _(pool):
                    for k, value in filled.items():
                        nc.gpsimd.memset(weights[k][:, :], value).then_inc(scaled, 1)

                @block.scalar
                def _(act):
                    act.wait_ge(small_loaded, 16 * SMALL)
                    for k in sels:
                        nc.scalar.activation(weights[k][:, :], sel_raw[k][:, :], ACT.Copy).then_inc(sel_rounded, 1)

                @block.vector
                def _(dve):
                    dve.wait_ge(small_loaded, 16 * SMALL)
                    nc.vector.tensor_scalar(weights["b2_half"][:, :], b2_row[:, :], 0.5, None, ALU.mult).then_inc(scaled, 1)
                    nc.vector.tensor_scalar(weights["gate_bias"][:, :], bias_raw[:, :], 1.0 / CAP, None, ALU.mult).then_inc(scaled, 1)

        ffn_phase(nc, "ffn1", x0, x1, weights)
        mlstm_phase(nc, x1, x2, seq, weights)
        ffn_phase(nc, "ffn2", x2, y, weights)




def kernel(**inputs):
    import numpy as np
    import concourse.bacc as bacc
    from concourse.bass_utils import run_bass_kernel_spmd

    args = {k.replace("L0_", ""): np.asarray(v) for k, v in inputs.items()}
    x = args["attn_x"]
    D = x.shape[2]
    NH, PARTS, F_ROW, I_ROW, GATES = 8, 128, 0, 32, 40

    def tiles(m):
        return np.ascontiguousarray(m.reshape(m.shape[0] // PARTS, PARTS, m.shape[1]).transpose(1, 0, 2).reshape(PARTS, -1))

    wgate = np.zeros((D, GATES), x.dtype)
    wgate[:, F_ROW:F_ROW + NH] = args["attn_Wf"].T
    wgate[:, I_ROW:I_ROW + NH] = args["attn_Wi"].T
    gate_bias = np.zeros((GATES, 1), x.dtype)
    gate_bias[F_ROW:F_ROW + NH, 0] = args["attn_bf"]
    gate_bias[I_ROW:I_ROW + NH, 0] = args["attn_bi"]

    s, t = np.arange(PARTS)[:, None], np.arange(PARTS)[None, :]
    sel_head = np.zeros((GATES, NH, PARTS), np.float32)
    sel_part = np.zeros((GATES, NH, PARTS // 4), np.float32)
    for h in range(NH):
        for r in (h, 32 + h):
            sel_head[r, h] = 1
            sel_part[r, h] = 1
    arrays = {
        "x": x,
        "wqk": tiles(np.concatenate([args["attn_Wq"].T, args["attn_Wk"].T], axis=1)),
        "wvo": tiles(np.concatenate([args["attn_Wv"].T, args["attn_Wog"].T], axis=1)),
        "wgate": tiles(wgate),
        "wout": tiles(args["attn_Wout"].T),
        "gate_bias": gate_bias,
        "ln_w": args["attn_ln_w"], "ln_b": args["attn_ln_b"],
        "u1": tiles(args["ffn_U1"]), "v1": args["ffn_V1"],
        "b1": np.ascontiguousarray(args["ffn_b1"].reshape(-1, PARTS).T),
        "u2": tiles(args["ffn_U2"]), "v2": args["ffn_V2"], "b2": args["ffn_b2"],
        "ident": np.eye(PARTS, dtype=np.float32),
        "mask": np.where(t >= s, 0, -1e30).astype(np.float32),
        "sel_head": sel_head.reshape(GATES, -1), "sel_part": sel_part.reshape(GATES, -1),
        "head_mask": (s // 32 == np.arange(4)[None, :]).astype(np.float32),
    }
    nc = bacc.Bacc("TRN2", target_bir_lowering=False, num_devices=1)
    fed, aps = {}, []
    for name, a in arrays.items():
        fed[f"in_{name}"] = np.ascontiguousarray(a)
        aps.append(nc.dram_tensor(f"in_{name}", a.shape, mybir.dt.from_np(a.dtype), kind="ExternalInput").ap())
    aps.append(nc.dram_tensor("out_x", x.shape, mybir.dt.from_np(x.dtype), kind="ExternalOutput").ap())
    macaron_kernel(nc, *aps)
    r = run_bass_kernel_spmd(nc, [fed], core_ids=[0])
    return r.results[0]["out_x"]
```

```python
from contextlib import ExitStack

import concourse.bass as bass
from concourse import mybir

P = 128
F32 = mybir.dt.float32
F32R = mybir.dt.float32r
ALU = mybir.AluOpType
ACT = mybir.ActivationFunctionType

LN_EPS = 1e-5
CELL_EPS = 1e-6
CAP = 15.0


class At:

    def __init__(self, pair, offset):
        self.pair, self.offset = pair, offset

    def __add__(self, k):
        return At(self.pair, self.offset + k)

    @property
    def parity(self):
        return self.offset % 2

    def count(self, per_step, more=0):
        return self.pair * (2 * per_step) + (self.offset * per_step + more)

    def turn(self):
        return self.pair + self.offset // 2


def as_f32(ap):
    return ap.bitcast(F32)


class Handover:

    def __init__(self, name, x, mv, veps, rstd, stats, half, eps, sem):
        self.x, self.mv, self.veps, self.rstd, self.stats, self.half, self.eps = x, mv, veps, rstd, stats, half, eps
        self.loaded = [sem(f"{name}_first_loaded{i}") for i in range(2)]
        self.raw, self.moments = sem(f"{name}_first_raw"), sem(f"{name}_first_moments")
        self.veps_done, self.rstd_done = sem(f"{name}_first_veps"), sem(f"{name}_first_rstd")

    def load(self, sp, view):
        for i in range(2):
            sp.dma_start(self.x[:, 2 * i:2 * i + 2], view[:, 2 * i:2 * i + 2]).then_inc(self.loaded[i], 16)

    def statistics(self, nc, dve):
        for j in range(4):
            if j % 2 == 0:
                dve.wait_ge(self.loaded[j // 2], 16)
            nc.vector.bn_stats(self.stats[:, j], self.x[:, j]).then_inc(self.raw, 1)
        for j in range(4):
            dve.wait_ge(self.raw, j + 1)
            nc.vector.bn_aggr(self.mv[:, j], self.stats[:, j]).then_inc(self.moments, 1)

    def deviation(self, nc, pool):
        pool.wait_ge(self.moments, 4)
        nc.gpsimd.tensor_tensor(self.veps[:, :], self.mv[:, :, 1], self.eps[:, :], ALU.add).then_inc(self.veps_done, 1)
        pool.wait_ge(self.veps_done, 1)
        nc.gpsimd.tensor_tensor(self.rstd[:, :], self.veps[:, :], self.half[:, :], ALU.pow).then_inc(self.rstd_done, 1)


class Staging:
    SLOTS = 5
    AHEAD = SLOTS - 1
    WIDTH = 512

    def __init__(self, nc, slots, sources, order, halved, sem):
        self.nc, self.slots, self.sources, self.halved = nc, slots, sources, halved
        self.place = {}
        self.parts = [(k, slice(a, min(a + self.WIDTH, sources[k].shape[1]))) for k, a in order]
        self.loaded = [sem(f"part_loaded{i}") for i in range(self.SLOTS)]
        self.rounded, self.split = sem("part_rounded"), sem("part_split")

    def first_of(self, k):
        return [m for m, _ in self.parts].index(k)

    def behind(self, k, column=None):
        column = self.sources[k].shape[1] - 1 if column is None else column
        return self.parts.index((k, next(c for m, c in self.parts if m == k and c.start <= column < c.stop))) + 1

    def slot(self, i):
        cols = self.parts[i][1]
        return self.slots[:, i % self.SLOTS, 0:cols.stop - cols.start]

    def load(self, act, i):
        k, cols = self.parts[i]
        if i >= self.SLOTS:
            act.wait_ge(self.split, i - self.SLOTS + 1)
        act.dma_start(self.slot(i), self.sources[k][:, cols]).then_inc(self.loaded[i % self.SLOTS], 16)

    def high(self, act, i):
        k, cols = self.parts[i]
        act.wait_ge(self.loaded[i % self.SLOTS], 16 * (i // self.SLOTS + 1))
        self.nc.scalar.activation(self.place[k][0][:, cols], self.slot(i), ACT.Copy, scale=0.5 if k in self.halved else 1.0)\
            .then_inc(self.rounded, 1)
        if i + self.AHEAD < len(self.parts):
            self.load(act, i + self.AHEAD)

    def low(self, dve, i):
        k, cols = self.parts[i]
        dve.wait_ge(self.rounded, i + 1)
        self.nc.vector.scalar_tensor_tensor(self.place[k][1][:, cols], self.slot(i), 0.5 if k in self.halved else 1.0,
                                            as_f32(self.place[k][0][:, cols]), ALU.mult, ALU.subtract).then_inc(self.split, 1)


def ffn_phase(nc, name, x_in, x_out, weights, staging, this, following, next_view, beside, stored, stored_before, at_act_end):
    T, D = x_in.shape
    TOK = 512
    TILES = TOK // P
    KD = D // P
    FT = staging.sources[f"{name} V1"].shape[1] // P
    NB = T // TOK
    RING = 4
    LAG = 3
    NORM_AT = 5
    TURN_AT = (10, 12, 13, 15)
    STATS_AT = (9, 10, 11, 13)
    P_BEFORE = 14
    O_AT = (1, 2, 4, 6)
    assert NB % 2 == 0 and NB >= 6 and FT == 16 and KD == 4

    src = x_in.rearrange("(n p j) d -> n p j d", p=P, j=TILES)
    dst = x_out.rearrange("(n p j) d -> n p j d", p=P, j=TILES)

    with ExitStack() as ctx:
        def sb(label, shape, dt=F32):
            return ctx.enter_context(nc.sbuf_tensor(f"{name}_{label}", shape, dt))

        def sem(label):
            return ctx.enter_context(nc.semaphore(f"{name}_{label}"))

        x_slot = (this.x, sb("x_odd", [P, TILES, D]))
        xb = sb("xb", [P, 2, TILES, D])
        xn = sb("xn", [P, TILES, D])
        xt_hi = sb("xt_hi", [P, KD, TOK], F32R)
        xt_lo = sb("xt_lo", [P, KD, TOK], F32R)
        y_out = weights["out_buffer"]
        p_hi, p_lo = sb("p_hi", [P, TOK], F32R), sb("p_lo", [P, TOK], F32R)
        q_hi, q_lo = sb("q_hi", [P, TOK], F32R), sb("q_lo", [P, TOK], F32R)
        h = sb("h", [P, RING, TOK])
        h_hi, h_lo = sb("h_hi", [P, RING, TOK], F32R), sb("h_lo", [P, RING, TOK], F32R)
        stats = sb("stats", [P, TILES, 6])
        mv = sb("mv", [P, TILES, 2])
        veps = sb("veps", [P, TILES])
        rstd = sb("rstd", [P, TILES])

        to_bank = [ctx.enter_context(nc.psum_tensor(f"{name}_to{i}", [P, 512], F32)) for i in range(2)]
        p_bank = ctx.enter_context(nc.psum_tensor(f"{name}_pb", [P, TOK], F32))
        q_bank = ctx.enter_context(nc.psum_tensor(f"{name}_qb", [P, TOK], F32))
        h_bank = [ctx.enter_context(nc.psum_tensor(f"{name}_hb{i}", [P, TOK], F32)) for i in range(RING)]

        loaded = [sem("loaded0"), sem("loaded1")]
        stats_raw, stats_done, veps_done, rstd_done = sem("stats_raw"), sem("stats_done"), sem("veps_done"), sem("rstd_done")
        xn_done, xb_done = sem("xn_done"), sem("xb_done")
        turned, xt_hi_done, xt_lo_done = sem("turned"), sem("xt_hi_done"), sem("xt_lo_done")
        p_done, p_hi_done, p_lo_done = sem("p_done"), sem("p_hi_done"), sem("p_lo_done")
        h_done, gelu_done, h_hi_done, h_lo_done = sem("h_done"), sem("gelu_done"), sem("h_hi_done"), sem("h_lo_done")
        h_used, q_hi_done, q_lo_done = sem("h_used"), sem("q_hi_done"), sem("q_lo_done")
        o_done, y_done = sem("o_done"), sem("y_done")

        (u1_hi, u1_lo), (v1_hi, v1_lo), (u2_hi, u2_lo), (v2_hi, v2_lo) = (staging.place[f"{name} {k}"] for k in ("U1", "V1", "U2", "V2"))
        split_here = beside is not None
        FIRST_PARTS = 3
        OWN_AT = [(0, 0), (0, 2), (0, 3), (0, 5), (0, 7), (0, 9), (0, 11)]
        BESIDE_AT = [(1, 0), (1, 3), (1, 12), (NB - 2, 0), (NB - 2, 3), (NB - 2, 9), (NB - 2, 12),
                     (NB - 1, 1), (NB - 1, 3), (NB - 1, 6), (NB - 1, 8), (NB - 1, 10), (NB - 1, 12)]
        beside_from = staging.first_of(beside) if split_here else None

        b1, b2_half, minus_half, ident = weights["b1"], weights["b2_half"], weights["minus_half"], weights["ident"]

        block = ctx.enter_context(nc.Block())

        def steps(eng, front, step):
            front(At(0, 0))
            step(At(0, 0), 0, True, True, True)
            step(At(0, 1), 1, False, True, True)
            with eng.Fori(0, NB // 2 - 2) as pair:
                for u in (2, 3):
                    step(At(pair, u), None, False, True, True)
            step(At(0, NB - 2), NB - 2, False, True, False)
            step(At(0, NB - 1), NB - 1, False, False, False)

        @block.sync
        def _(sp):
            def part(n, view):
                i = n.pair * 2 + n.offset
                return view[bass.ds(i, 1)].rearrange("a p j d -> (a p) j d")

            def load(n):
                sp.dma_start(x_slot[n.parity][:, :, :], part(n, src)).then_inc(loaded[n.parity], 16)

            def load_behind(n):
                sp.wait_ge(xn_done, n.count(TILES, TILES))
                sp.wait_ge(xb_done, n.count(TILES, TILES))
                load(n + 2)

            def store(n):
                sp.wait_ge(y_done, n.count(TILES, TILES))
                sp.dma_start(part(n, dst), y_out[:, :, :]).then_inc(stored, 16)

            load(At(0, 1))
            if stored_before is not None:
                sp.wait_ge(*stored_before)
            load_behind(At(0, 0))
            if split_here:
                for to, source in weights["late_rows"]:
                    sp.dma_start(to, source).then_inc(weights["late_loaded"], 16)
            load_behind(At(0, 1))
            with sp.Fori(0, NB // 2 - 2) as pair:
                for u in range(2):
                    store(At(pair, u))
                    load_behind(At(pair, u + 2))
            if following is not None:
                sp.wait_ge(xn_done, (NB - 1) * TILES)
                sp.wait_ge(xb_done, (NB - 1) * TILES)
                sp.wait_ge(stored, 16 * (NB - 4))
                following.load(sp, next_view)
            for n in range(NB - 4, NB):
                store(At(0, n))
            if following is None:
                sp.wait_ge(stored, 16 * NB)

        @block.gpsimd
        def _(pool):
            def front(n, first=False):
                pool.wait_ge(stats_done, (n + -1).count(TILES, TILES))
                nc.gpsimd.tensor_tensor(veps[:, :], mv[:, :, 1], weights["ln_eps"][:, 0:TILES], ALU.add).then_inc(veps_done, 1)
                pool.wait_ge(veps_done, (n + -1).count(1, 1))
                nc.gpsimd.tensor_tensor(rstd[:, :], veps[:, :], minus_half[:, 0:TILES], ALU.pow).then_inc(rstd_done, 1)
                if not first:
                    pool.wait_ge(y_done, (n + -1).count(TILES))
                with_bias(n)

            def with_bias(n):
                for j in range(TILES):
                    nc.gpsimd.tensor_tensor(xb[:, n.parity, j], x_slot[n.parity][:, j], b2_half[:, :], ALU.add)\
                        .then_inc(xb_done, 1)

            with_bias(At(0, 0))
            front(At(0, 1), first=True)
            with pool.Fori(0, NB // 2 - 1) as pair:
                for u in (2, 3):
                    front(At(pair, u))
            if following is not None:
                following.deviation(nc, pool)

        @block.scalar
        def _(act):
            def turn(n, k):
                act.wait_ge(turned, n.count(KD, k + 1))
                nc.scalar.activation(xt_hi[:, k], to_bank[k % 2][:, :], ACT.Copy).then_inc(xt_hi_done, 1)

            def p_evac(n):
                act.wait_ge(p_done, n.count(1, 1))
                nc.scalar.activation(p_hi[:, :], p_bank[:, :], ACT.Copy).then_inc(p_hi_done, 1)

            def front(n):
                if split_here:
                    staging.high(act, 0)
                for t in range(KD):
                    turn(n, t)
                if split_here:
                    staging.high(act, 1)
                p_evac(n)
                if split_here:
                    staging.high(act, 2)

            def step(n, number, first, ahead, stats_ahead):
                for j in range(FT):
                    act.wait_ge(h_done, n.count(FT, j + 1))
                    if j >= RING:
                        act.wait_ge(h_lo_done, n.count(FT, j + 1 - RING))
                    nc.scalar.activation(h[:, j % RING], h_bank[j % RING][:, :], ACT.Gelu_apprx_tanh, bias=b1[:, j:j + 1])\
                        .then_inc(gelu_done, 1)
                    act.wait_ge(gelu_done, n.count(FT, j + 1))
                    if j >= RING:
                        act.wait_ge(h_used, n.count(FT, j + 1 - RING))
                    nc.scalar.activation(h_hi[:, j % RING], h[:, j % RING], ACT.Copy).then_inc(h_hi_done, 1)
                    if ahead and j - 1 in TURN_AT:
                        turn(n + 1, TURN_AT.index(j - 1))
                    if split_here and (number, j) in OWN_AT:
                        staging.high(act, FIRST_PARTS + OWN_AT.index((number, j)))
                    if split_here and (number, j) in BESIDE_AT:
                        staging.high(act, beside_from + BESIDE_AT.index((number, j)))
                if ahead:
                    if TURN_AT[-1] == FT - 1:
                        turn(n + 1, KD - 1)
                    p_evac(n + 1)
                act.wait_ge(h_used, n.count(FT, FT))
                nc.scalar.activation(q_hi[:, :], q_bank[:, :], ACT.Copy).then_inc(q_hi_done, 1)

            steps(act, front, step)
            at_act_end()

        @block.vector
        def _(dve):
            def tile_stats(n, j):
                if j == 0:
                    dve.wait_ge(loaded[n.parity], (n.turn() + n.parity) * 16)
                nc.vector.bn_stats(stats[:, j], x_slot[n.parity][:, j]).then_inc(stats_raw, 1)

            def tile_moments(j):
                nc.vector.bn_aggr(mv[:, j], stats[:, j]).then_inc(stats_done, 1)

            def tile_norm(n, j):
                if j == 0:
                    dve.wait_ge(rstd_done, (n + -1).count(1, 1))
                    dve.wait_ge(turned, n.count(KD))
                nc.vector.tensor_scalar(xn[:, j], x_slot[n.parity][:, j], mv[:, j, 0:1], rstd[:, j:j + 1],
                                        ALU.subtract, ALU.mult).then_inc(xn_done, 1)

            def turn(n, k):
                dve.wait_ge(xt_hi_done, n.count(KD, k + 1))
                nc.vector.tensor_tensor(xt_lo[:, k], to_bank[k % 2][:, :], as_f32(xt_hi[:, k]), ALU.subtract)\
                    .then_inc(xt_lo_done, 1)

            def p_evac(n):
                dve.wait_ge(p_hi_done, n.count(1, 1))
                nc.vector.tensor_tensor(p_lo[:, :], p_bank[:, :], as_f32(p_hi[:, :]), ALU.subtract).then_inc(p_lo_done, 1)

            def residual(n, j):
                if j == 0:
                    dve.wait_ge(xb_done, n.count(TILES, TILES))
                    dve.wait_ge(stored, n.count(16))
                dve.wait_ge(o_done, n.count(TILES, j + 1))
                nc.vector.tensor_tensor(y_out[:, j], to_bank[j % 2][:, :], xb[:, n.parity, j], ALU.add)\
                    .then_inc(y_done, 1)

            def front(n):
                for j in range(TILES):
                    nc.vector.tensor_scalar(xn[:, j], this.x[:, j], this.mv[:, j, 0:1], this.rstd[:, j:j + 1],
                                            ALU.subtract, ALU.mult).then_inc(xn_done, 1)
                if split_here:
                    staging.low(dve, 0)
                for t in range(KD):
                    turn(n, t)
                    if t == 1:
                        next_statistics(n, 0)
                if split_here:
                    staging.low(dve, 1)
                next_statistics(n, 1)
                p_evac(n)
                if split_here:
                    staging.low(dve, 2)
                next_statistics(n, 2)
                next_statistics(n, 3)

            def next_statistics(n, j):
                tile_stats(n + 1, j)
                dve.wait_ge(stats_raw, j + 1)
                tile_moments(j)

            def step(n, number, first, ahead, stats_ahead):
                for j in range(FT):
                    moments_of = STATS_AT.index(j - 1) if stats_ahead and j - 1 in STATS_AT else None
                    if moments_of is not None:
                        dve.wait_ge(stats_raw, (n + 1).count(TILES, moments_of + 1))
                    dve.wait_ge(h_hi_done, n.count(FT, j + 1))
                    nc.vector.tensor_tensor(h_lo[:, j % RING], h[:, j % RING], as_f32(h_hi[:, j % RING]), ALU.subtract)\
                        .then_inc(h_lo_done, 1)
                    if moments_of is not None:
                        tile_moments(moments_of)
                    if stats_ahead and j in STATS_AT:
                        tile_stats(n + 2, STATS_AT.index(j))
                    if ahead and 0 <= j - NORM_AT < TILES:
                        tile_norm(n + 1, j - NORM_AT)
                    if ahead and j - 1 in TURN_AT:
                        turn(n + 1, TURN_AT.index(j - 1))
                    if not first and j in O_AT:
                        residual(n + -1, O_AT.index(j))
                    if split_here and (number, j) in OWN_AT:
                        staging.low(dve, FIRST_PARTS + OWN_AT.index((number, j)))
                    if split_here and (number, j) in BESIDE_AT:
                        staging.low(dve, beside_from + BESIDE_AT.index((number, j)))
                    if not ahead and following is not None and j == 7:
                        following.statistics(nc, dve)
                if ahead:
                    if TURN_AT[-1] == FT - 1:
                        turn(n + 1, KD - 1)
                    p_evac(n + 1)
                dve.wait_ge(q_hi_done, n.count(1, 1))
                nc.vector.tensor_tensor(q_lo[:, :], q_bank[:, :], as_f32(q_hi[:, :]), ALU.subtract).then_inc(q_lo_done, 1)
                if not ahead:
                    for j in range(TILES):
                        residual(n, j)

            steps(dve, front, step)

        @block.tensor
        def _(pe):
            def product(out, w_hi, w_lo, m_hi, m_lo, start, stop):
                nc.tensor.matmul(out, w_hi, m_hi, start=start, stop=False)
                nc.tensor.matmul(out, w_lo, m_hi, start=False, stop=False)
                return nc.tensor.matmul(out, w_hi, m_lo, start=False, stop=stop)

            def turn(n, k, first=False):
                if k == 0:
                    pe.wait_ge(xn_done, n.count(TILES, TILES))
                    if not first:
                        pe.wait_ge(y_done, (n + -1).count(TILES))
                if k >= 2:
                    pe.wait_ge(xt_lo_done, n.count(KD, k - 1))
                for j in range(TILES):
                    last = nc.tensor.transpose(to_bank[k % 2][:, j * P:(j + 1) * P], xn[:, j, k * P:(k + 1) * P], ident[:, :])
                last.then_inc(turned, 1)

            def p_product(n):
                pe.wait_ge(p_lo_done, n.count(1))
                for k in range(KD):
                    pe.wait_ge(xt_lo_done, n.count(KD, k + 1))
                    last = product(p_bank[:, :], u1_hi[:, k * P:(k + 1) * P], u1_lo[:, k * P:(k + 1) * P],
                                   xt_hi[:, k], xt_lo[:, k], k == 0, k == KD - 1)
                last.then_inc(p_done, 1)

            def h_product(n, j):
                if j == 0:
                    pe.wait_ge(p_lo_done, n.count(1, 1))
                if j >= RING:
                    pe.wait_ge(gelu_done, n.count(FT, j + 1 - RING))
                f = slice(j * P, (j + 1) * P)
                product(h_bank[j % RING][:, :], v1_hi[:, f], v1_lo[:, f], p_hi[:, :], p_lo[:, :], True, True)\
                    .then_inc(h_done, 1)

            def q_product(n, j):
                if j == 0:
                    pe.wait_ge(q_lo_done, n.count(1))
                pe.wait_ge(h_lo_done, n.count(FT, j + 1))
                r = slice(j * P, (j + 1) * P)
                last = product(q_bank[:, :], u2_hi[:, r], u2_lo[:, r], h_hi[:, j % RING], h_lo[:, j % RING],
                               j == 0, j == FT - 1)
                last.then_inc(h_used, 1)

            def o_product(n, j, behind_turn):
                if j == 0:
                    pe.wait_ge(q_lo_done, n.count(1, 1))
                if j < 2 and behind_turn:
                    pe.wait_ge(xt_lo_done, (n + 1).count(KD, KD - 1 + j))
                else:
                    pe.wait_ge(y_done, n.count(TILES, j - 1))
                t = slice(j * P, (j + 1) * P)
                product(to_bank[j % 2][:, :], q_hi[:, t], q_lo[:, t], v2_hi[:, :], v2_lo[:, :], True, True)\
                    .then_inc(o_done, 1)

            def front(n):
                for k in range(KD):
                    turn(n, k, first=True)
                if split_here:
                    pe.wait_ge(staging.split, 1)
                p_product(n)

            def step(n, number, first, ahead, stats_ahead):
                for j in range(FT + LAG):
                    if split_here and first and j < FT:
                        pe.wait_ge(staging.split, staging.behind(f"{name} V1", j * P))
                    if j < FT:
                        h_product(n, j)
                    if ahead and j - LAG == P_BEFORE:
                        p_product(n + 1)
                    if split_here and number == 1 and j in O_AT:
                        pe.wait_ge(staging.split, staging.behind(f"{name} V2"))
                    if not first and j in O_AT:
                        o_product(n + -1, O_AT.index(j), True)
                    if split_here and first and j >= LAG:
                        pe.wait_ge(staging.split, staging.behind(f"{name} U2", (j - LAG) * P))
                    if j >= LAG:
                        q_product(n, j - LAG)
                    if ahead and j in TURN_AT:
                        turn(n + 1, TURN_AT.index(j))
                if not ahead:
                    for j in range(TILES):
                        o_product(n, j, False)

            steps(pe, front, step)


def mlstm_phase(nc, x_in, x_out, seq, weights, staging, this, following, next_view, stored, stored_before, at_act_end):
    T, D = x_in.shape
    H = 8
    DK, DV = 32, D // H
    DV1 = DV + 1
    C = P
    TOK = 2 * C
    KD = D // P
    G = 2
    HG = H // G
    NS = T // TOK
    GATES = 40
    ROWS = 72
    QK_SCALE = float(DK) ** -0.5
    assert seq == 4 * TOK and NS % 2 == 0 and NS >= 4 and D == 512

    src = x_in.rearrange("(n c p) d -> n p c d", p=P, c=2)
    dst = x_out.rearrange("(n c p) d -> n p c d", p=P, c=2)

    with ExitStack() as ctx:
        def sb(label, shape, dt=F32):
            return ctx.enter_context(nc.sbuf_tensor(f"cell_{label}", shape, dt))

        def sem(label):
            return ctx.enter_context(nc.semaphore(f"cell_{label}"))

        def psum(label, shape):
            return ctx.enter_context(nc.psum_tensor(f"cell_{label}", shape, F32))

        staging.place["out"] = (sb("out_hi", [P, KD * D], F32R), sb("out_lo", [P, KD * D], F32R))
        w = staging.place

        ogw, ogb = sb("ogw", [P, 2, 2, D]), sb("ogb", [P, 2, 2, D])
        wt = sb("wt", [P, G, 2, HG * C])
        a = sb("a", [P, G, HG * C])

        sel_shapes = [weights[f"{k}_source"].shape for k in ("sel_head", "sel_part")]
        raw_sel_head, raw_sel_part = (sb(f"raw_sel{i}", shape) for i, shape in enumerate(sel_shapes))
        sel_head, sel_part = (sb(f"sel{i}", shape, F32R) for i, shape in enumerate(sel_shapes))
        x_ln = this.x[:, :, :].rearrange("p (u c) d -> p u c d", u=2)
        x_res, y_out = weights["out_buffer"][:, 0:2], weights["out_buffer"][:, 2:4]
        xt_hi, xt_lo = sb("xt_hi", [P, KD, TOK], F32R), sb("xt_lo", [P, KD, TOK], F32R)
        stats, mv, veps, rstd = sb("stats", [P, 2, 6]), sb("mv", [P, 2, 2]), sb("veps", [P, 2]), sb("rstd", [P, 2])
        q_s = sb("q_s", [P, G, TOK])
        q_bd = sb("q_bd", [P, G, 2, HG, C])
        q_d = sb("q_d", [P, 2, G, TOK])
        k_t = sb("k_t", [P, 2, G, TOK])
        k_w = sb("k_w", [P, 2, 2, H * DK])
        v1 = sb("v1", [P, 2, 2, H, DV1])
        og = sb("og", [P, D])
        gate = sb("gate", [H, 2, TOK])
        m_run = sb("m_run", [H, TOK + 1])
        log_f, d_sum = sb("log_f", [H, TOK]), sb("d_sum", [H, TOK])
        zeros = sb("zeros", [H, C])
        rows = sb("rows", [96, TOK])
        d_split = sb("d_split", [GATES, 2, TOK], F32R)
        cols = sb("cols", [P, 2, 2, ROWS])
        e_m = sb("e_m", [P, 2, 2, H])
        e_last = sb("e_last", [P, 2, H])
        e_d = sb("e_d", [P, 2, G, TOK])
        state = sb("state", [P, G, DV1])
        state_bd = sb("state_bd", [P, G, HG, DV1])
        den, rden = sb("den", [P, G, HG]), sb("rden", [P, G, HG])
        h, ho = sb("h", [P, D]), sb("ho", [P, D])
        h_stats, h_mv, h_veps, h_rstd = sb("h_stats", [P, 6]), sb("h_mv", [P, 2]), sb("h_veps", [P, 1]), sb("h_rstd", [P, 1])
        hot_hi, hot_lo = sb("hot_hi", [P, KD, C], F32R), sb("hot_lo", [P, KD, C], F32R)
        keep_m, keep_c = sb("keep_m", [H, 1]), sb("keep_c", [P, 1])

        wb = [psum(f"wb{i}", [P, 512]) for i in range(2)]
        gb = psum("gb", [P, 512])
        d_bc = psum("d_bc", [P, HG, TOK])
        s_b = psum("s_b", [P, 512])
        n_b = psum("n_b", [P, G, 512])
        og_bank = (wb[1], s_b)
        new_part = slice(HG * DV1, HG * DV1 + DV1)

        def xt_bank(b):
            return d_bc[:, 2 * b:2 * b + 2].rearrange("p h t -> p (h t)")


        names = """sel_loaded sel_rounded made stats_raw stats_done veps_done rstd_done xn_done turned xt_hi_done xt_lo_done
            gates_done tanh_done chain keep_m_done rows_turned cols_done e_cols_done exp_d_mm e_d_done
            q_mm q_done k_mm k_done v_mm v_done og_mm og_tanh_done og_done ogw_done kt_mm k_w_done q_d_done
            d_bc_done e_done wt_done s_done a_done n_done den_step h_done c_done keep_c_done keep_c_turned bd_done
            h_stats_raw h_stats_done h_veps_done h_rstd_done h_norm_done h_scaled_done ho_done
            hot_mm hot_hi_done hot_lo_done y_mm y_done res_loaded q_bd_done"""
        S = {k: sem(k) for k in names.split()}
        ln_loaded = [sem("ln_loaded0"), sem("ln_loaded1")]
        CHAIN = 14
        MADE = 9
        OUT_PARTS = range(staging.first_of("out"), staging.behind("out"))
        NEXT_PARTS = range(staging.first_of("ffn2 U1"), staging.behind("ffn2 V2"))

        mask, head_mask = weights["mask"], weights["head_mask"]
        ident, minus_half = weights["ident"], weights["minus_half"]

        block = ctx.enter_context(nc.Block())

        def steps(eng, front, step):
            front(At(0, 0))
            step(At(0, 0), True, True)
            with eng.Fori(0, NS // 2 - 2) as pair:
                for u in (1, 2):
                    step(At(pair, u), True, True)
            step(At(0, NS - 3), True, True)
            step(At(0, NS - 2), True, False)
            step(At(0, NS - 1), False, False)

        @block.sync
        def _(sp):
            def part(n, view):
                return view[bass.ds(n.pair * 2 + n.offset, 1)].rearrange("a p c d -> (a p) c d")

            def load_ln(n):
                sp.dma_start(x_ln[:, n.parity], part(n, src)).then_inc(ln_loaded[n.parity], 16)

            def load_res(n):
                sp.dma_start(x_res[:, :, :], part(n, src)).then_inc(S["res_loaded"], 16)

            def step(n, res, ln):
                if ln:
                    sp.wait_ge(S["turned"], (n + 1).count(2, 2))
                    load_ln(n + 3)
                sp.wait_ge(S["y_done"], n.count(2, 2))
                sp.dma_start(part(n, dst), y_out[:, :, :]).then_inc(stored, 16)
                if res:
                    load_res(n + 1)

            sp.dma_start(raw_sel_head[:, :], weights["sel_head_source"]).then_inc(S["sel_loaded"], 16)
            sp.dma_start(raw_sel_part[:, :], weights["sel_part_source"]).then_inc(S["sel_loaded"], 16)
            sp.wait_ge(*stored_before)
            load_res(At(0, 0))
            sp.wait_ge(S["turned"], 2)
            load_ln(At(0, 2))
            with sp.Fori(0, NS // 2 - 2) as pair:
                for u in range(2):
                    step(At(pair, u), True, True)
            for n in range(NS - 4, NS):
                if n == NS - 2:
                    sp.wait_ge(S["turned"], 2 * NS)
                    sp.wait_ge(stored, 16 * (NS - 2))
                    following.load(sp, next_view)
                step(At(0, n), n + 1 < NS, n + 3 < NS)

        @block.gpsimd
        def _(pool):
            nc.gpsimd.memset(state[:, :, :], 0.0).then_inc(S["made"], 1)
            nc.gpsimd.memset(state_bd[:, :, :, :], 0.0).then_inc(S["made"], 1)
            nc.gpsimd.memset(v1[:, :, :, :, :], 1.0).then_inc(S["made"], 1)
            nc.gpsimd.memset(rows[:, :], 0.0).then_inc(S["made"], 1)
            nc.gpsimd.memset(as_f32(d_split[:, :, :]), 0.0).then_inc(S["made"], 1)
            nc.gpsimd.memset(zeros[:, :], 0.0).then_inc(S["made"], 1)
            nc.gpsimd.memset(m_run[:, :], 0.0).then_inc(S["made"], 1)
            nc.gpsimd.memset(keep_m[:, :], 0.0).then_inc(S["made"], 1)
            nc.gpsimd.memset(keep_c[:, :], 0.0).then_inc(S["made"], 1)

            def x_rstd(n):
                pool.wait_ge(S["stats_done"], (n + -2).count(2, 2))
                nc.gpsimd.tensor_tensor(veps[:, :], mv[:, :, 1], weights["ln_eps"][:, 0:2], ALU.add).then_inc(S["veps_done"], 1)
                pool.wait_ge(S["veps_done"], (n + -2).count(1, 1))
                nc.gpsimd.tensor_tensor(rstd[:, :], veps[:, :], minus_half[:, 0:2], ALU.pow).then_inc(S["rstd_done"], 1)

            def out_gate(n, c):
                pool.wait_ge(S["og_done"], n.count(2, c + 1))
                nc.gpsimd.tensor_tensor(ogw[:, n.parity, c], og[:, :], weights["ln_w"][:, :], ALU.mult).then_inc(S["ogw_done"], 1)
                nc.gpsimd.tensor_tensor(ogb[:, n.parity, c], og[:, :], weights["ln_b"][:, :], ALU.mult).then_inc(S["ogw_done"], 1)

            def spread(n, c):
                if c == 1 and n.parity == 1:
                    pool.wait_ge(S["keep_c_done"], n.turn() + 1)
                for g in range(G):
                    pool.wait_ge(S["c_done"], n.count(4, 2 * c + g + 1))
                    nc.gpsimd.tensor_tensor(state_bd[:, g], state[:, g].unsqueeze(1).broadcast_to([P, HG, DV1]),
                                            head_mask[:, :].unsqueeze(2).broadcast_to([P, HG, DV1]), ALU.mult)\
                        .then_inc(S["bd_done"], 1)

            def h_rstd_of(n, c):
                pool.wait_ge(S["h_stats_done"], n.count(2, c + 1))
                nc.gpsimd.tensor_tensor(h_veps[:, :], h_mv[:, 1:2], weights["cell_eps"][:, 0:1], ALU.add).then_inc(S["h_veps_done"], 1)
                pool.wait_ge(S["h_veps_done"], n.count(2, c + 1))
                nc.gpsimd.tensor_tensor(h_rstd[:, :], h_veps[:, :], minus_half[:, 0:1], ALU.pow).then_inc(S["h_rstd_done"], 1)

            def front(n):
                out_gate(n, 0)
                out_gate(n, 1)

            def step(n, ahead, ln_ahead):
                if ln_ahead:
                    x_rstd(n + 2)
                elif ahead:
                    following.deviation(nc, pool)
                spread(n, 0)
                h_rstd_of(n, 0)
                if ahead:
                    out_gate(n + 1, 0)
                h_rstd_of(n, 1)
                spread(n, 1)
                if ahead:
                    out_gate(n + 1, 1)

            steps(pool, front, step)

        @block.scalar
        def _(act):
            def selectors():
                act.wait_ge(S["sel_loaded"], 32)
                nc.scalar.activation(sel_head[:, :], raw_sel_head[:, :], ACT.Copy).then_inc(S["sel_rounded"], 1)
                nc.scalar.activation(sel_part[:, :], raw_sel_part[:, :], ACT.Copy).then_inc(S["sel_rounded"], 1)

            def turn(n, first=False):
                if not first:
                    act.wait_ge(S["og_mm"], n.count(2))
                for b in range(2):
                    act.wait_ge(S["turned"], n.count(2, b + 1))
                    nc.scalar.activation(xt_hi[:, 2 * b:2 * b + 2], xt_bank(b), ACT.Copy).then_inc(S["xt_hi_done"], 1)

            def gate_tanh(n):
                act.wait_ge(S["gates_done"], n.count(1, 1))
                act.wait_ge(S["chain"], n.count(CHAIN))
                for i, r in enumerate((0, 32)):
                    nc.scalar.activation(gate[:, i], gb[r:r + H, 0:TOK], ACT.Tanh, bias=weights["gate_bias"][r:r + H, :],
                                         scale=1.0 / CAP).then_inc(S["tanh_done"], 1)

            def q_evac(n):
                act.wait_ge(S["q_mm"], n.count(1, 1))
                nc.scalar.activation(q_s[:, :], wb[0][:, :], ACT.Copy, scale=QK_SCALE).then_inc(S["q_done"], 1)

            def q_spread(n):
                act.wait_ge(S["q_done"], n.count(1, 1))
                act.wait_ge(S["s_done"], n.count(4))
                for j in range(HG):
                    nc.scalar.activation(q_bd[:, :, :, j], q_s[:, :, :].rearrange("p g (c t) -> p g c t", c=2), ACT.Copy,
                                         scale=head_mask[:, j:j + 1]).then_inc(S["q_bd_done"], 1)

            def k_evac(n):
                act.wait_ge(S["k_mm"], n.count(1, 1))
                nc.scalar.activation(k_t[:, n.parity], wb[1][:, :], ACT.Copy).then_inc(S["k_done"], 1)

            def v_evac(n, c):
                act.wait_ge(S["v_mm"], n.count(2, c + 1))
                nc.scalar.activation(v1[:, n.parity, c, :, 0:DV], wb[c][:, :].rearrange("p (h e) -> p h e", e=DV), ACT.Copy)\
                    .then_inc(S["v_done"], 1)

            def og_evac(n, c):
                act.wait_ge(S["og_mm"], n.count(2, c + 1))
                act.wait_ge(S["ogw_done"], n.count(4, 2 * c))
                nc.scalar.activation(og[:, :], og_bank[c][:, :], ACT.Tanh, scale=0.5).then_inc(S["og_tanh_done"], 1)

            def og_finish(n, c):
                act.wait_ge(S["og_tanh_done"], n.count(2, c + 1))
                nc.scalar.activation(og[:, :], og[:, :], ACT.Copy, scale=0.5, bias=0.5).then_inc(S["og_done"], 1)

            def e_cols(n):
                act.wait_ge(S["cols_done"], n.count(1, 1))
                nc.scalar.activation(e_last[:, :, :], cols[:, n.parity, :, 64:72], ACT.Exp).then_inc(S["e_cols_done"], 1)
                nc.scalar.activation(e_m[:, n.parity], cols[:, n.parity, :, 32:40], ACT.Exp, scale=-1.0).then_inc(S["e_cols_done"], 1)

            def e_d_evac(n):
                act.wait_ge(S["exp_d_mm"], n.count(1, 1))
                nc.scalar.activation(e_d[:, n.parity], wb[0][:, :], ACT.Exp).then_inc(S["e_d_done"], 1)

            def decay_weights(n, g):
                act.wait_ge(S["e_done"], n.count(4, 2 * g + 2))
                nc.scalar.activation(wt[:, g], wt[:, g], ACT.Exp).then_inc(S["wt_done"], 1)

            def hot_evac(n, c):
                act.wait_ge(S["hot_mm"], n.count(2, c + 1))
                nc.scalar.activation(hot_hi[:, :, :], wb[c][:, :], ACT.Copy).then_inc(S["hot_hi_done"], 1)

            def front(n):
                turn(n, first=True)
                act.wait_ge(weights["late_loaded"], 16 * weights["LATE"])
                gate_tanh(n)
                selectors()
                q_evac(n)
                k_evac(n)
                act.wait_ge(S["made"], MADE)
                v_evac(n, 0)
                e_cols(n)
                og_evac(n, 0)
                og_finish(n, 0)
                e_d_evac(n)
                for i in OUT_PARTS:
                    staging.high(act, i)
                q_spread(n)
                v_evac(n, 1)
                og_evac(n, 1)
                turn(n + 1)
                og_finish(n, 1)
                gate_tanh(n + 1)

            def step(n, ahead, ln_ahead):
                decay_weights(n, 0)
                if ahead:
                    q_evac(n + 1)
                if not ahead:
                    for i in NEXT_PARTS[0:1]:
                        staging.high(act, i)
                decay_weights(n, 1)
                if not ahead:
                    for i in NEXT_PARTS[1:8]:
                        staging.high(act, i)
                if ahead:
                    k_evac(n + 1)
                    v_evac(n + 1, 0)
                    e_cols(n + 1)
                    og_evac(n + 1, 0)
                    og_finish(n + 1, 0)
                    e_d_evac(n + 1)
                    v_evac(n + 1, 1)
                    q_spread(n + 1)
                hot_evac(n, 0)
                if not ahead:
                    for i in NEXT_PARTS[8:]:
                        staging.high(act, i)
                if ln_ahead:
                    turn(n + 2)
                if ahead:
                    og_evac(n + 1, 1)
                    og_finish(n + 1, 1)
                hot_evac(n, 1)
                if ln_ahead:
                    gate_tanh(n + 2)

            steps(act, front, step)
            at_act_end()

        @block.vector
        def _(dve):
            def x_stats(n):
                dve.wait_ge(ln_loaded[n.parity], n.turn() * 16)
                for j in range(2):
                    nc.vector.bn_stats(stats[:, j], x_ln[:, n.parity, j]).then_inc(S["stats_raw"], 1)
                dve.wait_ge(S["stats_raw"], (n + -2).count(2, 2))

            def x_moments(n):
                for j in range(2):
                    nc.vector.bn_aggr(mv[:, j], stats[:, j]).then_inc(S["stats_done"], 1)

            def x_norm(n):
                dve.wait_ge(S["rstd_done"], (n + -2).count(1, 1))
                for j in range(2):
                    nc.vector.tensor_scalar(x_ln[:, n.parity, j], x_ln[:, n.parity, j], mv[:, j, 0:1], rstd[:, j:j + 1],
                                            ALU.subtract, ALU.mult).then_inc(S["xn_done"], 1)

            def turn(n):
                for b in range(2):
                    dve.wait_ge(S["xt_hi_done"], n.count(2, b + 1))
                    ks = slice(2 * b, 2 * b + 2)
                    nc.vector.tensor_tensor(xt_lo[:, ks], xt_bank(b), as_f32(xt_hi[:, ks]), ALU.subtract)\
                        .then_inc(S["xt_lo_done"], 1)

            def gate_chain(n):
                links = [0]

                def link(ins):
                    links[0] += 1
                    ins.then_inc(S["chain"], 1)
                    dve.wait_ge(S["chain"], n.count(CHAIN, links[0]))

                f, i, m, m_prev = gate[:, 0], gate[:, 1], m_run[:, 1:TOK + 1], m_run[:, 0:TOK]
                dve.wait_ge(S["tanh_done"], n.count(2, 2))
                link(nc.vector.tensor_scalar(gate[:, :, :], gate[:, :, :], CAP, None, ALU.mult))
                if n.parity == 0:
                    link(nc.vector.tensor_scalar(m_run[:, 0:1], m_run[:, TOK:TOK + 1], keep_m[:, 0:1], None, ALU.mult))
                    nc.vector.tensor_scalar(keep_m[:, :], keep_m[:, :], -1.0, 1.0, ALU.mult, ALU.add).then_inc(S["keep_m_done"], 1)
                    dve.wait_ge(S["keep_m_done"], n.turn() + 1)
                else:
                    link(nc.vector.tensor_copy(m_run[:, 0:1], m_run[:, TOK:TOK + 1]))
                link(nc.vector.tensor_tensor_scan(m, f, i, m_run[:, 0:1], ALU.add, ALU.max))
                link(nc.vector.tensor_tensor(log_f[:, :], f, m_prev, ALU.add))
                link(nc.vector.tensor_tensor(log_f[:, :], log_f[:, :], m, ALU.subtract))
                link(nc.vector.tensor_tensor(i, i, m, ALU.subtract))
                for c in range(2):
                    t = slice(c * C, (c + 1) * C)
                    link(nc.vector.tensor_tensor_scan(d_sum[:, t], log_f[:, t], zeros[:, :], 0.0, ALU.add, ALU.add))
                link(nc.vector.tensor_tensor(rows[0:H, :], i, d_sum[:, :], ALU.subtract))
                link(nc.vector.tensor_copy(rows[32:32 + H, :], m))
                for c in range(2):
                    t = slice(c * C, (c + 1) * C)
                    last = (c + 1) * C - 1
                    link(nc.vector.tensor_scalar(rows[64:64 + H, t], rows[0:H, t], d_sum[:, last:last + 1], None, ALU.add))
                link(nc.vector.tensor_copy(d_split[0:H, n.parity], d_sum[:, :]))
                link(nc.vector.tensor_tensor(d_split[32:32 + H, n.parity], d_sum[:, :], as_f32(d_split[0:H, n.parity]), ALU.subtract))
                assert links[0] == CHAIN

            def cols_evac(n):
                dve.wait_ge(S["rows_turned"], n.count(1, 1))
                nc.vector.tensor_copy(cols[:, n.parity], gb[:, 256:256 + 2 * ROWS].rearrange("p (c r) -> p c r", c=2))\
                    .then_inc(S["cols_done"], 1)

            def k_weighted(n):
                dve.wait_ge(S["kt_mm"], n.count(1, 1))
                dve.wait_ge(S["e_cols_done"], n.count(2, 1))
                for c in range(2):
                    nc.vector.tensor_tensor(k_w[:, n.parity, c].rearrange("p (h e) -> p h e", e=DK),
                                            wb[0][:, c * 256:(c + 1) * 256].rearrange("p (h e) -> p h e", e=DK),
                                            e_last[:, c].unsqueeze(2).broadcast_to([P, H, DK]), ALU.mult)\
                        .then_inc(S["k_w_done"], 1)

            def q_decayed(n):
                dve.wait_ge(S["e_d_done"], n.count(1, 1))
                dve.wait_ge(S["q_done"], n.count(1, 1))
                nc.vector.tensor_tensor(q_d[:, n.parity], q_s[:, :], e_d[:, n.parity], ALU.mult).then_inc(S["q_d_done"], 1)

            def exponents(n, g):
                dve.wait_ge(S["d_bc_done"], n.count(2, g + 1))
                dve.wait_ge(S["cols_done"], n.count(1, 1))
                for c in range(2):
                    for j in range(HG):
                        r = g * HG + j
                        last = nc.vector.scalar_tensor_tensor(wt[:, g, c, j * C:(j + 1) * C], d_bc[:, j, c * C:(c + 1) * C],
                                                              cols[:, n.parity, c, r:r + 1], mask[:, :], ALU.add, ALU.min)
                    last.then_inc(S["e_done"], 1)

            def attend(n, c, g):
                dve.wait_ge(S["wt_done"], n.count(2, g + 1))
                dve.wait_ge(S["s_done"], n.count(4, 2 * c + g + 1))
                nc.vector.tensor_tensor(a[:, g], s_b[:, :], wt[:, g, c], ALU.mult).then_inc(S["a_done"], 1)

            def normalise(n, c):
                dve.wait_ge(S["n_done"], n.count(2, c + 1))
                dve.wait_ge(S["e_cols_done"], n.count(2, 2))
                num = n_b[:, :, 0:HG * DV1].rearrange("p g (h e) -> p g h e", e=DV1)
                qn = num[:, :, :, DV]
                nc.vector.scalar_tensor_tensor(den[:, :, :], qn, -1.0, e_m[:, n.parity, c].rearrange("p (g h) -> p g h", g=G),
                                               ALU.mult, ALU.max).then_inc(S["den_step"], 1)
                dve.wait_ge(S["den_step"], n.count(8, 4 * c + 1))
                nc.vector.tensor_tensor(den[:, :, :], qn, den[:, :, :], ALU.max).then_inc(S["den_step"], 1)
                dve.wait_ge(S["den_step"], n.count(8, 4 * c + 2))
                nc.vector.tensor_scalar(den[:, :, :], den[:, :, :], CELL_EPS, None, ALU.add).then_inc(S["den_step"], 1)
                dve.wait_ge(S["den_step"], n.count(8, 4 * c + 3))
                nc.vector.reciprocal(rden[:, :, :], den[:, :, :]).then_inc(S["den_step"], 1)
                dve.wait_ge(S["den_step"], n.count(8, 4 * c + 4))
                nc.vector.tensor_tensor(h[:, :].rearrange("p (g h e) -> p g h e", g=G, e=DV), num[:, :, :, 0:DV],
                                        rden[:, :, :].unsqueeze(3).broadcast_to([P, G, HG, DV]), ALU.mult)\
                    .then_inc(S["h_done"], 1)

            def update_state(n, c):
                for g in range(G):
                    last = (c + 1) * C - 1
                    nc.vector.scalar_tensor_tensor(state[:, g], state[:, g], e_d[:, n.parity, g, last:last + 1],
                                                   n_b[:, g, new_part], ALU.mult, ALU.add).then_inc(S["c_done"], 1)

            def keep_state(n):
                if n.parity == 1:
                    dve.wait_ge(S["c_done"], n.count(4, 4))
                    nc.vector.tensor_scalar(keep_c[:, :], keep_c[:, :], -1.0, 1.0, ALU.mult, ALU.add).then_inc(S["keep_c_turned"], 1)
                    dve.wait_ge(S["keep_c_turned"], n.turn() + 1)
                    nc.vector.tensor_scalar(state[:, :, :], state[:, :, :], keep_c[:, 0:1], None, ALU.mult).then_inc(S["keep_c_done"], 1)

            def h_statistics(n, c):
                dve.wait_ge(S["h_done"], n.count(2, c + 1))
                nc.vector.bn_stats(h_stats[:, :], h[:, :]).then_inc(S["h_stats_raw"], 1)
                dve.wait_ge(S["h_stats_raw"], n.count(2, c + 1))

            def h_moments():
                nc.vector.bn_aggr(h_mv[:, :], h_stats[:, :]).then_inc(S["h_stats_done"], 1)

            def gated(n, c):
                dve.wait_ge(S["h_rstd_done"], n.count(2, c + 1))
                nc.vector.tensor_scalar(h[:, :], h[:, :], h_mv[:, 0:1], h_rstd[:, 0:1], ALU.subtract, ALU.mult)\
                    .then_inc(S["h_norm_done"], 1)
                dve.wait_ge(S["h_norm_done"], n.count(2, c + 1))
                dve.wait_ge(S["ogw_done"], n.count(4, 2 * c + 2))
                nc.vector.tensor_tensor(h[:, :], h[:, :], ogw[:, n.parity, c], ALU.mult).then_inc(S["h_scaled_done"], 1)
                dve.wait_ge(S["h_scaled_done"], n.count(2, c + 1))
                nc.vector.tensor_tensor(ho[:, :], h[:, :], ogb[:, n.parity, c], ALU.add).then_inc(S["ho_done"], 1)

            def hot_evac(n, c):
                dve.wait_ge(S["hot_hi_done"], n.count(2, c + 1))
                nc.vector.tensor_tensor(hot_lo[:, :, :], wb[c][:, :], as_f32(hot_hi[:, :, :]), ALU.subtract)\
                    .then_inc(S["hot_lo_done"], 1)

            def residual(n, c):
                if c == 0:
                    dve.wait_ge(S["res_loaded"], n.count(16, 16))
                    dve.wait_ge(stored, n.count(16))
                dve.wait_ge(S["y_mm"], n.count(2, c + 1))
                nc.vector.tensor_tensor(y_out[:, c], wb[c][:, :], x_res[:, c], ALU.add).then_inc(S["y_done"], 1)

            def first_norm(n):
                for j in range(2):
                    r = 2 * n.offset + j
                    nc.vector.tensor_scalar(x_ln[:, n.parity, j], x_ln[:, n.parity, j], this.mv[:, r, 0:1], this.rstd[:, r:r + 1],
                                            ALU.subtract, ALU.mult).then_inc(S["xn_done"], 1)

            def front(n):
                first_norm(n)
                turn(n)
                first_norm(n + 1)
                dve.wait_ge(S["made"], MADE)
                gate_chain(n)
                cols_evac(n)
                k_weighted(n)
                q_decayed(n)
                for i in OUT_PARTS:
                    staging.low(dve, i)
                turn(n + 1)

            def step(n, ahead, ln_ahead):
                exponents(n, 0)
                exponents(n, 1)
                attend(n, 0, 0)
                if ln_ahead:
                    x_stats(n + 2)
                elif ahead:
                    following.statistics(nc, dve)
                else:
                    for i in NEXT_PARTS[0:3]:
                        staging.low(dve, i)
                attend(n, 0, 1)
                if ln_ahead:
                    x_moments(n + 2)
                if ahead:
                    gate_chain(n + 1)
                else:
                    for i in NEXT_PARTS[3:5]:
                        staging.low(dve, i)
                normalise(n, 0)
                if ahead:
                    cols_evac(n + 1)
                update_state(n, 0)
                attend(n, 1, 0)
                if ahead:
                    k_weighted(n + 1)
                h_statistics(n, 0)
                attend(n, 1, 1)
                h_moments()
                if ln_ahead:
                    x_norm(n + 2)
                gated(n, 0)
                if not ahead:
                    for i in NEXT_PARTS[5:8]:
                        staging.low(dve, i)
                    hot_evac(n, 0)
                normalise(n, 1)
                h_statistics(n, 1)
                update_state(n, 1)
                h_moments()
                if ahead:
                    hot_evac(n, 0)
                keep_state(n)
                gated(n, 1)
                if ln_ahead:
                    turn(n + 2)
                residual(n, 0)
                hot_evac(n, 1)
                if ahead:
                    q_decayed(n + 1)
                else:
                    for i in NEXT_PARTS[8:]:
                        staging.low(dve, i)
                residual(n, 1)

            steps(dve, front, step)

        @block.tensor
        def _(pe):
            def product(out, pairs):
                for i, (w_hi, w_lo, m_hi, m_lo) in enumerate(pairs):
                    nc.tensor.matmul(out, w_hi, m_hi, start=(i == 0), stop=False)
                    nc.tensor.matmul(out, w_lo, m_hi, start=False, stop=False)
                    last = nc.tensor.matmul(out, w_hi, m_lo, start=False, stop=(i == len(pairs) - 1))
                return last

            def turn(n):
                pe.wait_ge(S["xn_done"], n.count(2, 2))
                for b in range(2):
                    for k in (2 * b, 2 * b + 1):
                        for j in range(2):
                            last = nc.tensor.transpose(d_bc[:, k, j * P:(j + 1) * P],
                                                       x_ln[:, n.parity, j, k * P:(k + 1) * P], ident[:, :])
                    last.then_inc(S["turned"], 1)

            def gates(n):
                pe.wait_ge(S["xt_lo_done"], n.count(2, 2))
                pe.wait_ge(S["cols_done"], n.count(1))
                cols_of = [slice(k * GATES, (k + 1) * GATES) for k in range(KD)]
                product(gb[0:GATES, 0:TOK], [(w["gate"][0][:, s], w["gate"][1][:, s], xt_hi[:, k], xt_lo[:, k])
                                             for k, s in enumerate(cols_of)]).then_inc(S["gates_done"], 1)

            def qk_part(bank, n, base):
                for g in range(G):
                    at = [slice(k * 2 * G * P + base + g * P, k * 2 * G * P + base + (g + 1) * P) for k in range(KD)]
                    last = product(bank[:, g * TOK:(g + 1) * TOK],
                                   [(w["qk"][0][:, s], w["qk"][1][:, s], xt_hi[:, k], xt_lo[:, k]) for k, s in enumerate(at)])
                return last

            def q_proj(n):
                qk_part(wb[0], n, 0).then_inc(S["q_mm"], 1)

            def k_proj(n):
                qk_part(wb[1], n, G * P).then_inc(S["k_mm"], 1)

            def vo_part(bank, c, base):
                t = slice(c * C, (c + 1) * C)
                at = [slice(k * 2 * D + base, k * 2 * D + base + D) for k in range(KD)]
                return product(bank[:, :], [(xt_hi[:, k, t], xt_lo[:, k, t], w["vo"][0][:, s], w["vo"][1][:, s])
                                            for k, s in enumerate(at)])

            def v_proj(n, c):
                vo_part(wb[c], c, 0).then_inc(S["v_mm"], 1)

            def og_proj(n, c):
                vo_part(og_bank[c], c, D).then_inc(S["og_mm"], 1)

            def turn_rows(n):
                pe.wait_ge(S["chain"], n.count(CHAIN, CHAIN))
                for c in range(2):
                    last = nc.tensor.transpose(gb[:, 256 + c * ROWS:256 + (c + 1) * ROWS], rows[0:ROWS, c * C:(c + 1) * C],
                                               ident[0:ROWS, 0:ROWS])
                last.then_inc(S["rows_turned"], 1)

            def turn_k(n):
                pe.wait_ge(S["k_done"], n.count(1, 1))
                pe.wait_ge(S["v_done"], n.count(2, 1))
                for c in range(2):
                    for g in range(G):
                        last = nc.tensor.transpose(wb[0][:, c * 256 + g * P:c * 256 + (g + 1) * P],
                                                   k_t[:, n.parity, g, c * C:(c + 1) * C], ident[:, :])
                last.then_inc(S["kt_mm"], 1)

            def spread_d(n):
                pe.wait_ge(S["k_w_done"], n.count(2, 2))
                for g in range(G):
                    last = nc.tensor.matmul(wb[0][:, g * TOK:(g + 1) * TOK], sel_part[:, g * P:(g + 1) * P],
                                            d_split[:, n.parity], start=True, stop=True)
                last.then_inc(S["exp_d_mm"], 1)

            def broadcast_d(n, g):
                pe.wait_ge(S["e_done"], n.count(4, 2 * g))
                for j in range(HG):
                    r = g * HG + j
                    last = nc.tensor.matmul(d_bc[:, j], sel_head[:, r * P:(r + 1) * P], d_split[:, n.parity], start=True, stop=True)
                last.then_inc(S["d_bc_done"], 1)

            def scores(n, c, g):
                pe.wait_ge(S["a_done"], n.count(4, 2 * c + g))
                pe.wait_ge(S["q_bd_done"], n.count(HG, HG))
                last = nc.tensor.matmul(s_b[:, :], k_t[:, n.parity, g, c * C:(c + 1) * C],
                                        q_bd[:, g, c].rearrange("p h t -> p (h t)"), start=True, stop=True)
                last.then_inc(S["s_done"], 1)

            def numerator(n, c):
                pe.wait_ge(S["h_done"], n.count(2, c))
                pe.wait_ge(S["q_d_done"], n.count(1, 1))
                for g in range(G):
                    pe.wait_ge(S["bd_done"], n.count(4, 2 * c))
                    nc.tensor.matmul(n_b[:, g, 0:HG * DV1], q_d[:, n.parity, g, c * C:(c + 1) * C],
                                     state_bd[:, g].rearrange("p h e -> p (h e)"), start=True, stop=False)
                    pe.wait_ge(S["a_done"], n.count(4, 2 * c + g + 1))
                    for j in range(HG):
                        nc.tensor.matmul(n_b[:, g, j * DV1:(j + 1) * DV1], a[:, g, j * C:(j + 1) * C],
                                         v1[:, n.parity, c, g * HG + j], start=False, stop=(j == HG - 1))

            def state_product(n, c):
                for g in range(G):
                    for j in range(HG):
                        r = g * HG + j
                        last = nc.tensor.matmul(n_b[j * DK:(j + 1) * DK, g, new_part],
                                                k_w[:, n.parity, c, r * DK:(r + 1) * DK], v1[:, n.parity, c, r],
                                                start=True, stop=True)
                last.then_inc(S["n_done"], 1)

            def turn_h(n, c):
                pe.wait_ge(S["ho_done"], n.count(2, c + 1))
                for k in range(KD):
                    last = nc.tensor.transpose(wb[c][:, k * P:(k + 1) * P], ho[:, k * P:(k + 1) * P], ident[:, :])
                last.then_inc(S["hot_mm"], 1)

            def out_proj(n, c):
                pe.wait_ge(S["hot_lo_done"], n.count(2, c + 1))
                product(wb[c][:, :], [(hot_hi[:, k], hot_lo[:, k], w["out"][0][:, k * D:(k + 1) * D], w["out"][1][:, k * D:(k + 1) * D])
                                      for k in range(KD)]).then_inc(S["y_mm"], 1)

            def front(n):
                turn(n)
                gates(n)
                q_proj(n)
                k_proj(n)
                pe.wait_ge(S["q_done"], n.count(1, 1))
                v_proj(n, 0)
                turn_rows(n)
                turn_k(n)
                og_proj(n, 0)
                pe.wait_ge(S["sel_rounded"], 2)
                spread_d(n)
                pe.wait_ge(S["og_tanh_done"], n.count(2, 1))
                v_proj(n, 1)
                og_proj(n, 1)
                turn(n + 1)
                gates(n + 1)
                pe.wait_ge(staging.split, staging.behind("out"))
                pe.wait_ge(S["e_d_done"], 1)
                pe.wait_ge(S["v_done"], 2)

            def step(n, ahead, ln_ahead):
                f = n + 1
                if ahead:
                    pe.wait_ge(S["xt_lo_done"], f.count(2, 2))
                broadcast_d(n, 0)
                if ahead:
                    if n.offset:
                        pe.wait_ge(S["y_done"], n.count(2, -1))
                    q_proj(f)
                broadcast_d(n, 1)
                pe.wait_ge(S["og_tanh_done"], n.count(2, 2))
                scores(n, 0, 0)
                if ahead:
                    pe.wait_ge(S["y_done"], n.count(2))
                    k_proj(f)
                scores(n, 0, 1)
                if ahead:
                    pe.wait_ge(S["q_done"], f.count(1, 1))
                    v_proj(f, 0)
                numerator(n, 0)
                state_product(n, 0)
                scores(n, 1, 0)
                if ahead:
                    turn_k(f)
                    turn_rows(f)
                    pe.wait_ge(S["k_done"], f.count(1, 1))
                    og_proj(f, 0)
                scores(n, 1, 1)
                if ahead:
                    spread_d(f)
                    pe.wait_ge(S["og_tanh_done"], f.count(2, 1))
                    v_proj(f, 1)
                numerator(n, 1)
                state_product(n, 1)
                if ahead:
                    pe.wait_ge(S["e_d_done"], f.count(1, 1))
                else:
                    pe.wait_ge(S["y_done"], n.count(2, -1))
                turn_h(n, 0)
                if ln_ahead:
                    turn(n + 2)
                if ahead:
                    og_proj(f, 1)
                out_proj(n, 0)
                if ahead:
                    pe.wait_ge(S["v_done"], f.count(2, 2))
                else:
                    pe.wait_ge(S["y_done"], n.count(2))
                turn_h(n, 1)
                if ln_ahead:
                    gates(n + 2)
                out_proj(n, 1)

            steps(pe, front, step)


def macaron_kernel(nc, x, wqk, wvo, wgate, wout, gate_bias, ln_w, ln_b, u1, v1, b1, u2, v2, b2,
                   ident, mask, sel_head, sel_part, head_mask, out):
    Bs, seq, D = x.shape
    x0 = x.rearrange("b s d -> (b s) d")
    y = out.rearrange("b s d -> (b s) d")
    x1 = nc.dram_tensor("x_after_ffn1", [Bs * seq, D], F32, kind="Internal").ap()
    x2 = nc.dram_tensor("x_after_cell", [Bs * seq, D], F32, kind="Internal").ap()

    with ExitStack() as ctx:
        def sb(label, shape, dt=F32):
            return ctx.enter_context(nc.sbuf_tensor(label, shape, dt))

        def sem(label):
            return ctx.enter_context(nc.semaphore(label))

        ffn_parts = {"U1": u1, "V1": v1, "U2": u2, "V2": v2}
        cell_parts = {"gate": wgate, "qk": wqk, "vo": wvo, "out": wout}
        sources = {f"ffn1 {k}": d for k, d in ffn_parts.items()} | cell_parts | {f"ffn2 {k}": d for k, d in ffn_parts.items()}
        WIDTH = Staging.WIDTH

        def ffn_order(name):
            turns = [(f"{name} {k}", a) for a in range(0, v1.shape[1], WIDTH) for k in ("V1", "U2")]
            return [(f"{name} U1", 0)] + turns + [(f"{name} V2", 0)]

        order = ffn_order("ffn1") + [(k, a) for k, d in cell_parts.items() for a in range(0, d.shape[1], WIDTH)] + ffn_order("ffn2")
        staging = Staging(nc, sb("staging", [P, Staging.SLOTS, WIDTH]), sources, order, ("ffn1 V2", "ffn2 V2"), sem)
        for k in ("gate", "qk", "vo"):
            staging.place[k] = tuple(sb(f"{k}_{part}", [P, sources[k].shape[1]], F32R) for part in ("hi", "lo"))
        R, F = u1.shape[1], v1.shape[1]
        qk, vo = staging.place["qk"], staging.place["vo"]
        staging.place["ffn2 U1"] = tuple(t[:, 0:R] for t in qk)
        staging.place["ffn2 V2"] = tuple(t[:, R:R + v2.shape[1]] for t in qk)
        staging.place["ffn2 V1"] = tuple(t[:, 0:F] for t in vo)
        staging.place["ffn2 U2"] = tuple(t[:, F:F + u2.shape[1]] for t in vo)

        weights = {"out_buffer": sb("out_buffer", [P, 4, D])}
        rows = {"mask": (mask, [P, P]), "head_mask": (head_mask, [P, 4]), "ln_w": (ln_w, [P, D]), "ln_b": (ln_b, [P, D])}
        early = {"b2_half": (b2, [P, D]), "gate_bias": (gate_bias, [40, 1]), "ident": (ident, [P, P]), "b1": (b1, [P, b1.shape[1]])}
        TO_SCALE = ("b2_half", "gate_bias")
        for k, (_, shape) in (rows | early).items():
            weights[k] = sb(f"w_{k}", shape)
        filled = {"minus_half": -0.5, "ln_eps": LN_EPS, "cell_eps": CELL_EPS}
        for k in filled:
            weights[k] = sb(k, [P, 4])
        weights["sel_head_source"], weights["sel_part_source"] = sel_head, sel_part

        x_first, first_mv, first_stats = sb("x_first", [P, 4, D]), sb("first_mv", [P, 4, 2]), sb("first_stats", [P, 4, 6])
        first_veps, first_rstd = sb("first_veps", [P, 4]), sb("first_rstd", [P, 4])
        to_ffn1, to_cell, to_ffn2 = (Handover(k, x_first, first_mv, first_veps, first_rstd, first_stats, weights["minus_half"],
                                              weights["ln_eps"], sem) for k in ("ffn1", "cell", "ffn2"))

        def ffn_view(t):
            return t[0:4 * P].rearrange("(p j) d -> p j d", j=4)

        scaled_loaded, early_loaded, filled_done, scaled = sem("scaled_loaded"), sem("early_loaded"), sem("filled_done"), sem("scaled")
        late = [(weights[k][:, :], d.partition_broadcast(P) if len(d.shape) == 1 else d) for k, (d, _) in rows.items()]
        weights["late_rows"], weights["LATE"], weights["late_loaded"] = late, len(late), sem("late_loaded")

        table_seed, table_asked = sb("table_seed", [P, 1]), sem("table_asked")

        def ask_for_table(function):
            nc.scalar.activation(table_seed[:, :], weights["minus_half"][:, 0:1], function).then_inc(table_asked, 1)

        with nc.Block() as block:
            @block.sync
            def _(sp):
                to_ffn1.load(sp, ffn_view(x0))

            @block.gpsimd
            def _(pool):
                for k, value in filled.items():
                    nc.gpsimd.memset(weights[k][:, :], value).then_inc(filled_done, 1)
                for k, (d, _) in early.items():
                    d = d.partition_broadcast(P) if len(d.shape) == 1 else d
                    pool.dma_start(weights[k][:, :], d).then_inc(scaled_loaded if k in TO_SCALE else early_loaded, 16)
                pool.wait_ge(filled_done, len(filled))
                to_ffn1.deviation(nc, pool)

            @block.scalar
            def _(act):
                for i in range(Staging.AHEAD):
                    staging.load(act, i)
                act.wait_ge(filled_done, len(filled))
                ask_for_table(ACT.Gelu_apprx_tanh)
                act.wait_ge(early_loaded, 16 * (len(early) - len(TO_SCALE)))

            @block.vector
            def _(dve):
                to_ffn1.statistics(nc, dve)
                dve.wait_ge(scaled_loaded, 16 * len(TO_SCALE))
                nc.vector.tensor_scalar(weights["b2_half"][:, :], weights["b2_half"][:, :], 0.5, None, ALU.mult).then_inc(scaled, 1)
                nc.vector.tensor_scalar(weights["gate_bias"][:, :], weights["gate_bias"][:, :], 1.0 / CAP, None, ALU.mult).then_inc(scaled, 1)

        stored = [sem(f"stored{i}") for i in range(3)]
        NB, NS = Bs * seq // 512, Bs * seq // 256
        cell_view = x1[0:4 * P].rearrange("(n p) d -> p n d", p=P)
        with ExitStack() as first:
            for k, d in ffn_parts.items():
                staging.place[f"ffn1 {k}"] = tuple(first.enter_context(nc.sbuf_tensor(f"{k}_{part}", [P, d.shape[1]], F32R))
                                                   for part in ("hi", "lo"))
            ffn_phase(nc, "ffn1", x0, x1, weights, staging, to_ffn1, to_cell, cell_view, "gate", stored[0], None,
                      lambda: ask_for_table(ACT.Exp))
        mlstm_phase(nc, x1, x2, seq, weights, staging, to_cell, to_ffn2, ffn_view(x2), stored[1], (stored[0], 16 * NB),
                    lambda: ask_for_table(ACT.Gelu_apprx_tanh))
        ffn_phase(nc, "ffn2", x2, y, weights, staging, to_ffn2, None, None, None, stored[2], (stored[1], 16 * NS), lambda: None)




def kernel(**inputs):
    import numpy as np
    import concourse.bacc as bacc
    from concourse.bass_utils import run_bass_kernel_spmd

    args = {k.replace("L0_", ""): np.asarray(v) for k, v in inputs.items()}
    x = args["attn_x"]
    D = x.shape[2]
    NH, PARTS, F_ROW, I_ROW, GATES = 8, 128, 0, 32, 40

    def tiles(m):
        return np.ascontiguousarray(m.reshape(m.shape[0] // PARTS, PARTS, m.shape[1]).transpose(1, 0, 2).reshape(PARTS, -1))

    wgate = np.zeros((D, GATES), x.dtype)
    wgate[:, F_ROW:F_ROW + NH] = args["attn_Wf"].T
    wgate[:, I_ROW:I_ROW + NH] = args["attn_Wi"].T
    gate_bias = np.zeros((GATES, 1), x.dtype)
    gate_bias[F_ROW:F_ROW + NH, 0] = args["attn_bf"]
    gate_bias[I_ROW:I_ROW + NH, 0] = args["attn_bi"]

    s, t = np.arange(PARTS)[:, None], np.arange(PARTS)[None, :]
    sel_head = np.zeros((GATES, NH, PARTS), np.float32)
    sel_part = np.zeros((GATES, NH, PARTS // 4), np.float32)
    for h in range(NH):
        for r in (h, 32 + h):
            sel_head[r, h] = 1
            sel_part[r, h] = 1
    arrays = {
        "x": x,
        "wqk": tiles(np.concatenate([args["attn_Wq"].T, args["attn_Wk"].T], axis=1)),
        "wvo": tiles(np.concatenate([args["attn_Wv"].T, args["attn_Wog"].T], axis=1)),
        "wgate": tiles(wgate),
        "wout": tiles(args["attn_Wout"].T),
        "gate_bias": gate_bias,
        "ln_w": args["attn_ln_w"], "ln_b": args["attn_ln_b"],
        "u1": tiles(args["ffn_U1"]), "v1": args["ffn_V1"],
        "b1": np.ascontiguousarray(args["ffn_b1"].reshape(-1, PARTS).T),
        "u2": tiles(args["ffn_U2"]), "v2": args["ffn_V2"], "b2": args["ffn_b2"],
        "ident": np.eye(PARTS, dtype=np.float32),
        "mask": np.where(t >= s, 0, -1e30).astype(np.float32),
        "sel_head": sel_head.reshape(GATES, -1), "sel_part": sel_part.reshape(GATES, -1),
        "head_mask": (s // 32 == np.arange(4)[None, :]).astype(np.float32),
    }
    nc = bacc.Bacc("TRN2", target_bir_lowering=False, num_devices=1)
    fed, aps = {}, []
    for name, a in arrays.items():
        fed[f"in_{name}"] = np.ascontiguousarray(a)
        aps.append(nc.dram_tensor(f"in_{name}", a.shape, mybir.dt.from_np(a.dtype), kind="ExternalInput").ap())
    aps.append(nc.dram_tensor("out_x", x.shape, mybir.dt.from_np(x.dtype), kind="ExternalOutput").ap())
    macaron_kernel(nc, *aps)
    r = run_bass_kernel_spmd(nc, [fed], core_ids=[0])
    return r.results[0]["out_x"]
```
